# Optimizing a Trainium2 kernel written in Bass

```python
import numpy as np
import jax
import jax.numpy as jnp

def _softmax(x, axis=-1):
    return jax.nn.softmax(x, axis=axis)

def _gelu(x):
    return jax.nn.gelu(x, approximate=True)

def _silu(x):
    return jax.nn.silu(x)

def _sigmoid(x):
    return jax.nn.sigmoid(x)

def _layernorm(x, axis=-1, eps=1e-05):
    m = jnp.mean(x, axis=axis, keepdims=True)
    v = jnp.var(x, axis=axis, keepdims=True)
    return (x - m) / jnp.sqrt(v + eps)

def _scatter_add(tgt, idx, src, axis=0):
    return tgt.at[idx].add(src)

def _segment_sum(src, seg, n):
    return jax.ops.segment_sum(src, seg, n)
kernel_name = 'mk_gnn_ffn_d2_gnn_r8_99e1e2'

def setup_inputs(seed: int=0):
    np.random.seed(seed)
    _w = jnp.asarray

    def _rec_inputs():
        import jax
        import jax.numpy as jnp
        _gk = jax.random.key(seed)
        x = -6.415e-05 + 1 * jax.random.normal(jax.random.fold_in(_gk, 1), (1250, 512), jnp.float32)
        src = jax.random.randint(jax.random.fold_in(_gk, 2), (20000,), 0, 1250, jnp.int32)
        dst = jax.random.randint(jax.random.fold_in(_gk, 3), (20000,), 0, 1250, jnp.int32)
        _o = jnp.argsort(dst, stable=True)
        src = src[_o]
        dst = dst[_o]
        return (x, src, dst)
    x, src, dst = _rec_inputs()

    def _L0_gnn_setup():
        import jax, jax.numpy as jnp
        import numpy as np
        N = 2500
        E = 31250
        B = 128
        Fin = 512
        Fqk = 512
        Fv = 512
        H = 8
        key = jax.random.key(seed)
        k1, k2, k3, k4 = jax.random.split(key, 4)
        x = jax.random.normal(k1, (N, Fin), dtype=jnp.float32)
        batch = jnp.sort(jax.random.randint(k2, (N,), 0, B)).astype(jnp.int32)
        ei = jax.random.randint(k3, (2, E), 0, N).astype(jnp.int32)
        W = jax.random.normal(k4, (Fin, 2 * Fqk + Fv), dtype=jnp.float32) / np.sqrt(Fin).astype(np.float32)
        return {'x': x, 'batch': batch, 'ei': ei, 'W': W}
    _L0_gnn_all = _L0_gnn_setup()
    _L0_gnn_in = {k: v for k, v in _L0_gnn_all.items() if k in ('W',)}
    del _L0_gnn_all

    def _L0_ffn_setup():
        import jax, jax.numpy as jnp
        import numpy as np
        E = 8
        K = 2
        D = 512
        H = 256
        EPS = 1e-06

        def _rmsnorm(x, w):
            return x * jax.lax.rsqrt(jnp.mean(x * x, axis=-1, keepdims=True) + EPS) * w
        key = jax.random.key(seed)
        ks = jax.random.split(key, 5)
        B, T = (4, 256)
        x = jax.random.normal(ks[0], (B, T, D), dtype=jnp.float32)
        gate_w = jax.random.normal(ks[1], (D, E), dtype=jnp.float32) / np.sqrt(D)
        w1 = jax.random.normal(ks[2], (E, D, H), dtype=jnp.float32) / np.sqrt(D)
        w2 = jax.random.normal(ks[3], (E, H, H), dtype=jnp.float32) / np.sqrt(H)
        w3 = jax.random.normal(ks[4], (E, H, D), dtype=jnp.float32) / np.sqrt(H)
        n1 = jnp.ones((E, H), dtype=jnp.float32)
        n2 = jnp.ones((E, H), dtype=jnp.float32)
        return {'x': x, 'gate_w': gate_w, 'w1': w1, 'w2': w2, 'w3': w3, 'n1': n1, 'n2': n2}
    _L0_ffn_all = _L0_ffn_setup()
    _L0_ffn_in = {k: v for k, v in _L0_ffn_all.items() if k in ('gate_w', 'w1', 'w2', 'w3', 'n1', 'n2')}
    del _L0_ffn_all

    def _L1_gnn_setup():
        import jax, jax.numpy as jnp
        import numpy as np
        N_NODES = 6250
        N_EDGES = 50000
        D = 512
        LN_EPS = 1e-05
        key = jax.random.key(seed)
        k0, k1, k2, k3 = jax.random.split(key, 4)
        x = jax.random.normal(k0, (N_NODES, D), dtype=jnp.float32)
        src = jax.random.randint(k1, (N_EDGES,), 0, N_NODES, dtype=jnp.int64)
        dst = jax.random.randint(k2, (N_EDGES,), 0, N_NODES, dtype=jnp.int64)
        W = jax.random.normal(k3, (D, D), dtype=jnp.float32) * 0.05
        b = jnp.zeros((D,), dtype=jnp.float32)
        gamma = jnp.ones((D,), dtype=jnp.float32)
        beta = jnp.zeros((D,), dtype=jnp.float32)
        return {'x': x, 'W': W, 'b': b, 'gamma': gamma, 'beta': beta, 'src': src, 'dst': dst}
    _L1_gnn_all = _L1_gnn_setup()
    _L1_gnn_in = {k: v for k, v in _L1_gnn_all.items() if k in ('W', 'b', 'gamma', 'beta')}
    del _L1_gnn_all

    def _L1_ffn_setup():
        import jax, jax.numpy as jnp
        import numpy as np
        EPS = 1e-09
        LN_EPS = 1e-05

        def _layernorm(x, gamma):
            x = x.astype(jnp.float32)
            mu = jnp.mean(x, axis=-1, keepdims=True)
            var = jnp.var(x, axis=-1, keepdims=True)
            return (x - mu) * jax.lax.rsqrt(var + LN_EPS) * gamma
        key = jax.random.key(seed)
        ks = jax.random.split(key, 5)
        b, n, d, e, h = (4, 1024, 512, 6, 256)
        x = jax.random.normal(ks[0], (b, n, d), dtype=jnp.float32)
        w_gating = jax.random.normal(ks[1], (d, e), dtype=jnp.float32)
        std1 = 1.0 / np.sqrt(h)
        std2 = 1.0 / np.sqrt(d)
        w1 = jax.random.uniform(ks[2], (e, d, h), jnp.float32, -std1, std1)
        w2 = jax.random.uniform(ks[3], (e, h, d), jnp.float32, -std2, std2)
        gamma = jnp.ones((d,), dtype=jnp.float32)
        return {'x': x, 'w_gating': w_gating, 'gamma': gamma, 'w1': w1, 'w2': w2}
    _L1_ffn_all = _L1_ffn_setup()
    _L1_ffn_in = {k: v for k, v in _L1_ffn_all.items() if k in ('w_gating', 'gamma', 'w1', 'w2')}
    del _L1_ffn_all
    return {'x': x, 'src': src, 'dst': dst, 'L0_gnn_W': _L0_gnn_in['W'], 'L0_ffn_gate_w': _L0_ffn_in['gate_w'], 'L0_ffn_w1': _L0_ffn_in['w1'], 'L0_ffn_w2': _L0_ffn_in['w2'], 'L0_ffn_w3': _L0_ffn_in['w3'], 'L0_ffn_n1': _L0_ffn_in['n1'], 'L0_ffn_n2': _L0_ffn_in['n2'], 'L1_gnn_W': _L1_gnn_in['W'], 'L1_gnn_b': _L1_gnn_in['b'], 'L1_gnn_gamma': _L1_gnn_in['gamma'], 'L1_gnn_beta': _L1_gnn_in['beta'], 'L1_ffn_w_gating': _L1_ffn_in['w_gating'], 'L1_ffn_gamma': _L1_ffn_in['gamma'], 'L1_ffn_w1': _L1_ffn_in['w1'], 'L1_ffn_w2': _L1_ffn_in['w2']}

def reference(x, src, dst, L0_gnn_W, L0_ffn_gate_w, L0_ffn_w1, L0_ffn_w2, L0_ffn_w3, L0_ffn_n1, L0_ffn_n2, L1_gnn_W, L1_gnn_b, L1_gnn_gamma, L1_gnn_beta, L1_ffn_w_gating, L1_ffn_gamma, L1_ffn_w1, L1_ffn_w2):
    import jax
    import jax.numpy as jnp

    def _L0_gnn_ref(x, batch, ei, W):
        import jax, jax.numpy as jnp
        import numpy as np
        N = 2500
        E = 31250
        B = 128
        Fin = 512
        Fqk = 512
        Fv = 512
        H = 8
        src, dest = (ei[0], ei[1])
        n = x.shape[0]
        Fh = Fqk // H
        Fhv = Fv // H
        scaling = float(Fh) ** (-0.5)
        qkv = x @ W
        q, k, v = jnp.split(qkv, [Fqk, 2 * Fqk], axis=-1)
        q = (q * scaling).reshape(n, H, Fh)
        k = k.reshape(n, H, Fh)
        v = v.reshape(n, H, Fhv)
        qs = q[src]
        ks = k[dest]
        vs = v[dest]
        aw = jnp.einsum('ehf,ehf->eh', qs, ks)
        m = jax.ops.segment_max(aw, src, num_segments=n)
        e = jnp.exp(aw - m[src])
        denom = jax.ops.segment_sum(e, src, num_segments=n)
        alpha = e / denom[src]
        out = jax.ops.segment_sum(alpha[:, :, None] * vs, src, num_segments=n)
        return out.reshape(n, Fv)

    def _L0_ffn_ref(x, gate_w, w1, w2, w3, n1, n2):
        import jax, jax.numpy as jnp
        import numpy as np
        E = 8
        K = 2
        D = 512
        H = 256
        EPS = 1e-06

        def _rmsnorm(x, w):
            return x * jax.lax.rsqrt(jnp.mean(x * x, axis=-1, keepdims=True) + EPS) * w
        B, T, Dm = x.shape
        xf = x.reshape(-1, Dm)
        logits = xf @ gate_w
        tk_logits, tk_idx = jax.lax.top_k(logits, K)
        gates = jax.nn.softmax(tk_logits, axis=-1)
        h1 = jax.nn.gelu(jnp.einsum('nd,edh->enh', xf, w1), approximate=False)
        h1 = _rmsnorm(h1, n1[:, None, :])
        h2 = jax.nn.gelu(jnp.einsum('enh,ehk->enk', h1, w2), approximate=False)
        h2 = _rmsnorm(h2, n2[:, None, :])
        expert_out = jnp.einsum('enh,ehd->ned', h2 + h1, w3)
        sel = jnp.take_along_axis(expert_out, tk_idx[:, :, None], axis=1)
        out = jnp.sum(gates[:, :, None] * sel, axis=1)
        return out.reshape(B, T, Dm)

    def _L1_gnn_ref(x, W, b, gamma, beta, src, dst):
        import jax, jax.numpy as jnp
        import numpy as np
        N_NODES = 6250
        N_EDGES = 50000
        D = 512
        LN_EPS = 1e-05
        n = x.shape[0]
        ones = jnp.ones(src.shape, dtype=x.dtype)
        deg_out = jnp.clip(jax.ops.segment_sum(ones, src, num_segments=n), 1.0)
        deg_in = jnp.clip(jax.ops.segment_sum(ones, dst, num_segments=n), 1.0)
        h = x * jax.lax.rsqrt(deg_out)[:, None]
        agg = jax.ops.segment_sum(h[src], dst, num_segments=n)
        h = agg * jax.lax.rsqrt(deg_in)[:, None]
        h = h @ W + b
        mu = jnp.mean(h, axis=-1, keepdims=True)
        var = jnp.mean(jnp.square(h - mu), axis=-1, keepdims=True)
        h = (h - mu) * jax.lax.rsqrt(var + LN_EPS) * gamma + beta
        return jax.nn.gelu(h, approximate=False)

    def _L1_ffn_ref(x, w_gating, gamma, w1, w2):
        import jax, jax.numpy as jnp
        import numpy as np
        EPS = 1e-09
        LN_EPS = 1e-05

        def _layernorm(x, gamma):
            x = x.astype(jnp.float32)
            mu = jnp.mean(x, axis=-1, keepdims=True)
            var = jnp.var(x, axis=-1, keepdims=True)
            return (x - mu) * jax.lax.rsqrt(var + LN_EPS) * gamma
        b, n, d = x.shape
        E = w_gating.shape[-1]
        C = max(min(n, int(n * 6.0 / E)), 4)
        raw = jnp.einsum('bnd,de->bne', x, w_gating)
        probs = jax.nn.softmax(raw, axis=-1)
        gate1 = jnp.max(probs, axis=-1)
        idx1 = jnp.argmax(probs, axis=-1)
        mask1 = jax.nn.one_hot(idx1, E, dtype=jnp.float32)
        gates_wo1 = probs * (1.0 - mask1)
        gate2 = jnp.max(gates_wo1, axis=-1)
        denom = gate1 + gate2 + EPS
        gate1 = gate1 / denom
        pos1 = (jnp.cumsum(mask1, axis=-2) - mask1) * mask1
        mask1 = mask1 * (pos1 < float(C)).astype(jnp.float32)
        mask1_flat = jnp.sum(mask1, axis=-1)
        pos1_flat = jnp.sum(pos1, axis=-1).astype(jnp.int32)
        gate1 = gate1 * mask1_flat
        combine = gate1[..., None, None] * mask1_flat[..., None, None] * jax.nn.one_hot(idx1, E, dtype=jnp.float32)[..., None] * jax.nn.one_hot(pos1_flat, C, dtype=jnp.float32)[..., None, :]
        dispatch = (combine != 0).astype(jnp.float32)
        expert_in = jnp.einsum('bnd,bnec->ebcd', x, dispatch)
        xn = _layernorm(expert_in, gamma)
        hidden = jax.nn.gelu(jnp.einsum('ebcd,edh->ebch', xn, w1), approximate=False)
        expert_out = jnp.einsum('ebch,ehd->ebcd', hidden, w2)
        out = jnp.einsum('ebcd,bnec->bnd', expert_out, combine)
        return out
    edge_index = jnp.stack([src, dst])
    batch0 = jnp.zeros((1250,), jnp.int32)
    x = x + _L0_gnn_ref(_layernorm(x, axis=-1), batch0, edge_index, L0_gnn_W)
    x = x + _L0_ffn_ref(_layernorm(x, axis=-1)[None], L0_ffn_gate_w, L0_ffn_w1, L0_ffn_w2, L0_ffn_w3, L0_ffn_n1, L0_ffn_n2)[0]
    x = x + _L1_gnn_ref(_layernorm(x, axis=-1), L1_gnn_W, L1_gnn_b, L1_gnn_gamma, L1_gnn_beta, src, dst)
    x = x + _L1_ffn_ref(_layernorm(x, axis=-1)[None], L1_ffn_w_gating, L1_ffn_gamma, L1_ffn_w1, L1_ffn_w2)[0]
    return x

_drawn_inputs = setup_inputs


def setup_inputs(seed=0):
    import zlib

    import numpy as np

    out = dict(_drawn_inputs(seed))
    spreads = {'L0_ffn_n1': (1.0, 0.2),
     'L0_ffn_n2': (1.0, 0.2),
     'L1_gnn_b': (0.0, 0.1),
     'L1_gnn_gamma': (1.0, 0.2),
     'L1_gnn_beta': (0.0, 0.1),
     'L1_ffn_gamma': (1.0, 0.6)}
    factors = {}
    for name, (base, spread) in spreads.items():
        noise = np.random.default_rng([zlib.crc32(name.encode()), seed]).standard_normal(out[name].shape)
        drawn = base * np.exp(spread * noise) if base else spread * noise
        out[name] = jnp.asarray(drawn.astype(out[name].dtype))
    for name, factor in factors.items():
        out[name] = (out[name] * factor).astype(out[name].dtype)
    return out
```

```python
from contextlib import ExitStack

import concourse.bass as bass
from concourse import mybir

F32 = mybir.dt.float32
BF16 = mybir.dt.bfloat16
I32 = mybir.dt.int32
U32 = mybir.dt.uint32
U16 = mybir.dt.uint16
ALU = mybir.AluOpType
ACT = mybir.ActivationFunctionType
X_AXIS = mybir.AxisListType.X

N, E = 1250, 20000
P, T = 125, 10
D, C = 512, 4
HEADS, DH = 8, 64
EP, ET = 125, 160
HALF = N // 2
SHIFT = 12
WIN = 20
GEN_WIN = 32
GROUP = 4
NEG = -1.0e30
BIG = 10000.0
TM = 128
E0, H0, K0 = 8, 256, 2
MT0 = (K0 * N + E0 * (TM - 1)) // TM
E1, H1 = 6, 256
MT1 = (N + E1 * (TM - 1)) // TM
LANES = 3
LN_EPS, RMS_EPS, GATE_EPS = 1e-5, 1e-6, 1e-9
assert E == EP * ET and N == P * T and MT0 % LANES == 0 and MT1 % LANES == 0
assert WIN * EP < 2 ** SHIFT and GEN_WIN * EP < 2 ** SHIFT and ET % GEN_WIN == 0
PIECES = ((0, 512), (512, 1024), (1024, N))
TPIECES = ((0, 4), (4, 8), (8, 10))


def above_zero(eng, sem, value):
    if not (isinstance(value, int) and value <= 0):
        eng.wait_ge(sem, value)


def gnn_moe_kernel(nc, x, src, dst, L0_gnn_W, L0_ffn_gate_w, L0_ffn_w1, L0_ffn_w2, L0_ffn_w3,
                   L0_ffn_n1, L0_ffn_n2, L1_gnn_W, L1_gnn_b, L1_gnn_gamma, L1_gnn_beta,
                   L1_ffn_w_gating, L1_ffn_gamma, L1_ffn_w1, L1_ffn_w2, out):
    counts_d = nc.dram_tensor("counts_d", (N, N), F32).ap()
    logs_d = nc.dram_tensor("logs_d", (N, N), F32).ap()
    slots0_d = nc.dram_tensor("slots0_d", (MT0 * TM, D), F32).ap()
    slots1_d = nc.dram_tensor("slots1_d", (MT1 * TM, D), F32).ap()
    made0_d = nc.dram_tensor("made0_d", (MT0 * TM, D), F32).ap()
    made1_d = nc.dram_tensor("made1_d", (MT1 * TM, D), F32).ap()

    with ExitStack() as ctx:
        def sb(name, shape, dt=F32):
            return ctx.enter_context(nc.sbuf_tensor(name, shape, dt))

        def sem(name):
            return ctx.enter_context(nc.semaphore(name))

        X = sb("X", [P, T, D])
        XN = sb("XN", [P, T, D])
        XT = sb("XT", [128, C, N])
        R_W = sb("R_W", [128, 6144])
        R_B = sb("R_B", [128, 22500])
        R_A = sb("R_A", [128, 7680])
        Wqkv = R_W[:, :].rearrange("p (c n) -> p c n", c=C)
        QT = R_B[:, 0:5000].rearrange("p (j n) -> p j n", j=4)
        KT = R_B[:, 5000:10000].rearrange("p (j n) -> p j n", j=4)
        LNB = [R_B[0:P, 10000 + 1250 * b:10000 + 1250 * b + N] for b in range(2)]
        SC = [R_A[0:P, 1250 * b:1250 * b + N] for b in range(2)]
        PR = [R_A[0:P, 2500 + 1250 * b:2500 + 1250 * b + N] for b in range(2)]
        PT = [R_A[0:P, 5000 + 1250 * b:5000 + 1250 * b + N].rearrange("p (j n) -> p j n", j=T)
              for b in range(2)]
        oh_src = R_B[0:EP, 0:GROUP * HALF // 2].bitcast(BF16).rearrange("p (g n) -> p g n", g=GROUP)
        oh_dst = R_B[0:EP, 1250:1250 + GROUP * P // 2].bitcast(BF16).rearrange("p (g n) -> p g n", g=GROUP)
        iota_src = R_B[0:EP, 1500:1500 + 314].bitcast(U16)[:, 0:HALF]
        iota_dst = R_B[0:EP, 1820:1820 + 64].bitcast(U16)[:, 0:P]
        raw_idx = R_B[0:80, 2000:2500].bitcast(I32).rearrange("p (k e) -> p k e", k=2)
        idx_f = R_B[0:80, 2500:3250].rearrange("p (k e) -> p k e", k=3)
        src_f = R_B[0:80, 3250:3500]
        upper = R_B[0:80, 3500:3750]
        span_diag = R_B[0:80, 3750:4070].rearrange("p (k q) -> p k q", k=4)
        span_tmp = R_B[0:T, 4100:4100 + 5 * ET].rearrange("p (k t) -> p k t", k=5)
        packed = R_A[0:P, 0:HALF].bitcast(I32)
        unpacked = R_A[0:P, 650:650 + N].bitcast(I32)
        CT = R_A[0:P, 1900:1900 + N]
        lnCT = R_A[0:P, 3150:3150 + N]
        penalty = R_A[0:P, 4400:4400 + N]
        stage = R_A[0:P, 5650:5650 + N].rearrange("p (i n) -> p i n", i=T)
        idxT = R_B[0:EP, 6300:6300 + 3 * ET].rearrange("p (k t) -> p k t", k=3)
        win = R_B[0:EP, 6800:6800 + 3 * GEN_WIN].rearrange("p (k t) -> p k t", k=3)
        zero_rows = R_B[:, 7000:7512]
        ln_stage = R_B[0:P, 12500:12500 + N].rearrange("p (i n) -> p i n", i=T)
        sumCT = R_B[0:P, 5000:5000 + N]
        W1E = R_B[:, 0:8192].rearrange("p (e n) -> p e n", e=E0)
        W2E = R_B[:, 8192:12288].rearrange("p (e n) -> p e n", e=E0)
        W3E = R_B[:, 12288:20480].rearrange("p (e n) -> p e n", e=E0)
        N1B = R_W[:, 0:2048]
        N2B = R_W[:, 2048:4096]
        WG = R_W[:, 4096:6144].rearrange("p (c n) -> p c n", c=C)

        def lane(off, n):
            return [R_A[:, 2560 * k + off:2560 * k + off + n] for k in range(LANES)]

        xs, xsT, act1, h1n, h2n, hT, ys = (lane(0, 512), lane(512, 512), lane(1024, 256), lane(1280, 256),
                                           lane(1536, 256), lane(1792, 256), lane(2048, 512))
        CS = R_B[0:P, 10000:22500].rearrange("p (i n) -> p i n", i=T)
        BIAS, GAMMA, BETA = (R_B[:, 6144 + 512 * k:6656 + 512 * k] for k in range(3))
        AGG = [R_A[0:P, 512 * k:512 * k + 512] for k in range(2)]
        AGT = [R_A[:, 1024 + 512 * k:1536 + 512 * k].rearrange("p (c n) -> p c n", c=C) for k in range(2)]
        HG = [R_A[0:P, 2048 + 512 * k:2560 + 512 * k] for k in range(2)]
        W1B = R_B[:, 0:6144].rearrange("p (e n) -> p e n", e=E1)
        GAM1 = R_B[:, 7680:8192]
        W2B = R_B[:, 10000:16144].rearrange("p (e n) -> p e n", e=E1)
        rows = [R_A[0:P, 512 * k:512 * k + 512] for k in range(8)]

        ident = sb("ident", [128, 128])
        zeros_b = sb("zeros_b", [1, 640], BF16)
        Qst = R_W[:, 0:4 * P].rearrange("p (j n) -> p j n", j=4)
        tile_off = sb("tile_off", [128, T])
        bounds = sb("bounds", [80, 4])
        spans = sb("spans", [T, 8])
        ctl_f = sb("ctl_f", [1, 32])
        ctl = sb("ctl", [1, 32], I32)
        deg_in = sb("deg_in", [P, T])
        deg_part = sb("deg_part", [P, T])
        deg_out = sb("deg_out", [P, T])
        has_edge = sb("has_edge", [P, T])
        inv_in = sb("inv_in", [P, T])
        inv_out = sb("inv_out", [P, T])
        neg_max = sb("neg_max", [P, 4])
        den = sb("den", [P, 2])
        rden = sb("rden", [P, 2])
        head_out = R_W[0:P, 512:640].rearrange("p (b n) -> p b n", b=2)
        stats = sb("stats", [128, T, 6])
        mv = sb("mv", [128, T, 2])
        rstd = sb("rstd", [128, T])
        half_pow = sb("half_pow", [128, T])
        before = sb("before", [128, 128])
        ones = sb("ones", [128, 128])
        gate_w = sb("gate_w", [128, C, 8])
        logits = R_A[0:P, 6900:6980].rearrange("p (a b) -> p a b", a=10)
        top = R_A[0:P, 6980:7060].rearrange("p (a b) -> p a b", a=10)
        top_i = R_A[0:P, 7060:7140].bitcast(U32).rearrange("p (a b) -> p a b", a=10)
        pick = R_A[0:P, 7140:7160].rearrange("p (a b) -> p a b", a=10)
        iota8 = sb("iota8", [P, 8])
        iotaT = sb("iotaT", [1, MT0])
        mask = R_A[0:P, 7160:7400].rearrange("p (a b c) -> p a b c", a=3, b=10)
        place = R_A[0:128, 7400:7480].rearrange("p (a b) -> p a b", a=10)
        cnt = sb("cnt", [128, 5, 8])
        cnt_i = sb("cnt_i", [128, 8], I32)
        owner = R_B[0:1, 20500:20500 + 8 * MT0].rearrange("p (t e) -> p t e", e=8)
        owner_f = sb("owner_f", [1, MT0])
        owner_i = sb("owner_i", [1, MT0], I32)
        slot_f = sb("slot_f", [P, 2, T])
        slot = sb("slot", [P, 2, T], I32)
        gates = sb("gates", [P, 4, T])
        sq = [R_B[:, 20800 + H0 * k:20800 + H0 * k + H0] for k in range(LANES)]
        ssum = sb("ssum", [128, LANES])
        rms = sb("rms", [128, LANES])

        ps = ctx.enter_context(nc.psum_tensor("ps", [128, 8 * 512], F32))

        def bank(b, rows=128, cols=512, off=0):
            return ps[0:rows, 512 * b + off:512 * b + off + cols]

        names = """x_in edges_in w_in wg_in consts zero_made zeros_out
            idx_step idx_turned span_step diag_made span_sums ctl_sums ctl_ready
            win_made hot slots_free gen_win gen_hot gen_free gen_step
            packed_out unpacked_out ct_made max_made pen_made ln_made lnct_made
            ct_turned lnct_turned ct_moved lnct_moved counts_out
            degs_made ln_stat ln_rstd xn_made xt_turned xt_moved v_turned v_moved
            qk_made qk_moved q_staged s_made z_made p_made p_turned pt_moved_a pt_moved_v o_made o_moved
            rden_made x_added x_stored
            gate_in w1e_in w2e_in w3e_in nrm_in log_made mask_made rank_made rank_step
            slot_made gate_step gate_exp rows_out xs_in0 xs_in1 xs_in2 xs_turned xs_moved h1_made g1_made
            ss_made rms_step rms_made n1_made h1_turned h1_moved h2_made g2_made ss2_made rms2_step
            rms2_made h2_scaled n2_made h2_turned h2_moved y_made y_moved y_out0 y_out1 y_out2
            counts_in logs_out vec_in hs_made agg_made agg_moved agg_turned agt_moved hg_made hg_biased
            hg_stat hg_rstd hg_pow hg_shift hg_gelu
            gate1_in w1b_in w2b_in gam_in log1_made g1_step g1_exp rank1_made rank1_step
            log1_top slot1_made rows1_out z_in0 z_in1 z_in2 z_turned z_moved hh_made gg_made gg_turned
            gg_moved yy_made yy_moved yy_out0 yy_out1 yy_out2
            out_done chain dchain degi_made"""
        s = {n: sem(n) for n in names.split()}
        rows_in = [sem(f"rows_in{k}") for k in range(8)]

        def S(n):
            return s[n]

        block = ctx.enter_context(nc.Block())

        logs_in = [sem("logs_in0"), sem("logs_in1")]
        xs_in = [s["xs_in0"], s["xs_in1"], s["xs_in2"]]
        y_out = [s["y_out0"], s["y_out1"], s["y_out2"]]
        z_in = [s["z_in0"], s["z_in1"], s["z_in2"]]
        yy_out = [s["yy_out0"], s["yy_out1"], s["yy_out2"]]
        @block.sync
        def _(sp):
            sp.dma_start(raw_idx[:, 0, :], dst.rearrange("(q e) -> q e", q=80)).then_inc(S("edges_in"), 16)
            sp.dma_start(raw_idx[:, 1, :], src.rearrange("(q e) -> q e", q=80)).then_inc(S("edges_in"), 16)
            sp.dma_start(X[:, :, :], x.rearrange("(i p) d -> p i d", p=P)).then_inc(S("x_in"), 16)
            sp.dma_start(Wqkv, L0_gnn_W.rearrange("(c p) n -> p c n", c=C)).then_inc(S("w_in"), 16)
            sp.dma_start(gate_w[:, :, :], L0_ffn_gate_w.rearrange("(c p) n -> p c n", c=C)).then_inc(S("gate_in"), 16)
            sp.wait_ge(S("zero_made"), 1)
            for d, n in ((slots0_d, MT0), (slots1_d, MT1)):
                sp.dma_start(d.rearrange("(t p) d -> p t d", p=TM),
                             zero_rows.unsqueeze(1).to_broadcast([TM, n, D])).then_inc(S("zeros_out"), 16)

            def store_counts(b):
                sp.wait_ge(S("ct_moved"), 3 * b + 3)
                sp.dma_start(counts_d[:, bass.ds(b * P, P)].rearrange("(i p) d -> p i d", p=P),
                             stage).then_inc(S("counts_out"), 16)
                sp.wait_ge(S("lnct_moved"), 3 * b + 3)
                sp.dma_start(logs_d[:, bass.ds(b * P, P)].rearrange("(i p) d -> p i d", p=P),
                             ln_stage).then_inc(S("logs_out"), 16)
            with sp.Fori(0, T) as b:
                store_counts(b)

            def load_logs(i, b, guard):
                if guard:
                    sp.wait_ge(S("z_made"), i * HEADS - HEADS)
                sp.dma_start(LNB[b], logs_d[bass.ds(i * P, P), :]).then_inc(logs_in[b], 16)
            sp.wait_ge(S("logs_out"), 16 * T)
            load_logs(0, 0, False)
            load_logs(1, 1, False)
            with sp.Fori(1, T // 2) as ii:
                load_logs(2 * ii, 0, True)
                load_logs(2 * ii + 1, 1, True)
            sp.wait_ge(S("x_added"), T * HEADS)
            for e in range(E0):
                sp.dma_start(W1E[:, e, :].rearrange("p (c n) -> p c n", c=C),
                             L0_ffn_w1[e].rearrange("(c p) n -> p c n", c=C)).then_inc(S("w1e_in"), 16)
            for n_, dest in ((L0_ffn_n1, N1B), (L0_ffn_n2, N2B)):
                sp.dma_start(dest, n_.rearrange("e h -> (e h)").partition_broadcast(128)).then_inc(S("nrm_in"), 16)
            for e in range(E0):
                sp.dma_start(W2E[:, e, :].rearrange("p (c n) -> p c n", c=2),
                             L0_ffn_w2[e].rearrange("(c p) n -> p c n", c=2)).then_inc(S("w2e_in"), 16)
                sp.dma_start(W3E[:, e, :].rearrange("p (c n) -> p c n", c=2),
                             L0_ffn_w3[e].rearrange("(c p) n -> p c n", c=2)).then_inc(S("w3e_in"), 16)
            sp.dma_start(WG, L1_gnn_W.rearrange("(c p) n -> p c n", c=C)).then_inc(S("wg_in"), 16)

            def mix_loads(slots, made, groups, ins, turned, outs, moved):
                def load(t, k, wait):
                    if wait is not None:
                        sp.wait_ge(turned, wait)
                    sp.dma_start(xs[k][:, :], slots[bass.ds(t * TM, TM), :]).then_inc(ins[k], 16)

                def store(t, k, g):
                    sp.wait_ge(moved, g * LANES + k + 1)
                    sp.dma_start(made[bass.ds(t * TM, TM), :], ys[k][:, :]).then_inc(outs[k], 16)
                for k in range(LANES):
                    load(k, k, None)
                with sp.Fori(0, groups - 1) as g:
                    for k in range(LANES):
                        load(g * LANES + LANES + k, k, g * LANES + k + 1)
                    for k in range(LANES):
                        store(g * LANES + k, k, g)
                for k in range(LANES):
                    store((groups - 1) * LANES + k, k, groups - 1)
            sp.wait_ge(S("rows_out"), 16 * K0 * T)
            mix_loads(slots0_d, made0_d, MT0 // LANES, xs_in, S("xs_turned"), y_out, S("y_moved"))
            sp.wait_ge(S("y_made"), MT0)
            sp.wait_ge(S("counts_out"), 16 * T)
            sp.dma_start(CS, counts_d.rearrange("(i p) d -> p i d", p=P)).then_inc(S("counts_in"), 16)
            for v, dest in ((L1_gnn_b, BIAS), (L1_gnn_gamma, GAMMA), (L1_gnn_beta, BETA)):
                sp.dma_start(dest, v.partition_broadcast(128)).then_inc(S("vec_in"), 16)
            for e in range(E1):
                sp.dma_start(W1B[:, e, :].rearrange("p (c n) -> p c n", c=C),
                             L1_ffn_w1[e].rearrange("(c p) n -> p c n", c=C)).then_inc(S("w1b_in"), 16)
            sp.dma_start(GAM1, L1_ffn_gamma.partition_broadcast(128)).then_inc(S("gam_in"), 16)
            sp.wait_ge(S("log_made"), 1)
            sp.dma_start(gate_w[:, :, 0:E1], L1_ffn_w_gating.rearrange("(c p) n -> p c n", c=C))\
              .then_inc(S("gate1_in"), 16)
            sp.wait_ge(S("agg_made"), T)
            for e in range(E1):
                sp.dma_start(W2B[:, e, :].rearrange("p (c n) -> p c n", c=2),
                             L1_ffn_w2[e].rearrange("(c p) n -> p c n", c=2)).then_inc(S("w2b_in"), 16)
            sp.wait_ge(S("rows1_out"), 16 * T)
            mix_loads(slots1_d, made1_d, MT1 // LANES, z_in, S("z_turned"), yy_out, S("yy_moved"))
            for i in range(T):
                sp.wait_ge(S("x_stored"), i + 1)
                sp.dma_start(out[P * i:P * i + P, :], X[:, i, :]).then_inc(S("out_done"), 16)
            sp.wait_ge(S("out_done"), 16 * T)
            sp.wait_ge(S("zeros_out"), 32)

        @block.tensor
        def _(pe):
            pe.wait_ge(S("consts"), 1)
            pe.wait_ge(S("idx_step"), 5)
            for k in range(3):
                for r in range(2):
                    ins = pe.transpose(bank(6, EP, 80, (2 * k + r) * 80), idx_f[:, k, EP * r:EP * r + EP],
                                       ident[0:80, 0:80])
            ins.then_inc(S("idx_turned"), 1)
            pe.wait_ge(S("diag_made"), 4)
            pe.matmul(bank(7, T, 320), ones[0:80, 0:T], span_diag.rearrange("p k q -> p (k q)"),
                      start=True, stop=True).then_inc(S("span_sums"), 1)
            pe.wait_ge(S("span_step"), 8)
            for k in range(2):
                ins = pe.matmul(bank(7, 1, T, 320 + 16 * k), spans[:, 6 + k:7 + k], ident[0:T, 0:T],
                                start=True, stop=True)
            ins.then_inc(S("ctl_sums"), 1)
            pe.wait_ge(S("ctl_ready"), 1)
            all_hold = pe.value_load(ctl[0:1, T:T + 1], min_val=0, max_val=1)

            def count_group(g0, buf, hot, free, first=False, last=False):
                for k in range(GROUP):
                    pe.wait_ge(hot, g0 + k + 1)
                    a, z = first and k == 0, last and k == GROUP - 1
                    pe.matmul(bank(2 * buf, P, 512), oh_dst[:, k, :], oh_src[:, k, 0:512], start=a, stop=z,
                              skip_group_check=True)
                    pe.matmul(bank(2 * buf + 1, P, HALF - 512), oh_dst[:, k, :], oh_src[:, k, 512:HALF],
                              start=a, stop=z, skip_group_check=True).then_inc(free, 1)

            def count_window(g0, tiles, buf, *sems):
                count_group(g0, buf, *sems, first=True)
                with pe.Fori(1, tiles // GROUP - 1) as k:
                    count_group(g0 + k * GROUP, buf, *sems)
                count_group(g0 + (tiles - GROUP), buf, *sems, last=True)

            def turn_counts(b):
                for sourced, source, turned, moved in ((S("ct_made"), CT, S("ct_turned"), S("ct_moved")),
                                                       (S("lnct_made"), lnCT, S("lnct_turned"), S("lnct_moved"))):
                    pe.wait_ge(sourced, b + 1)
                    if source is CT:
                        above_zero(pe, S("lnct_moved"), 3 * b)
                    else:
                        pe.wait_ge(S("ct_moved"), 3 * b + 3)
                    for q, (a, z) in enumerate(TPIECES):
                        for i in range(a, z):
                            ins = pe.transpose(bank(4 + q, P, P, (i - a) * P), source[:, i * P:i * P + P],
                                               ident[0:P, 0:P])
                        ins.then_inc(turned, 1)

            def fast_block(b, buf, after):
                above_zero(pe, S("packed_out"), b - 1)
                count_window(b * WIN, WIN, buf, S("hot"), S("slots_free"))
                if after is not None:
                    turn_counts(after)

            with pe.If(all_hold):
                pe.nop().then_inc(S("slots_free"), GROUP)
                fast_block(0, 0, None)
                fast_block(1, 1, 0)
                with pe.Fori(2, T, 2) as b:
                    fast_block(b, 0, b - 1)
                    fast_block(b + 1, 1, b)
                turn_counts(T - 1)
            with pe.Else():
                pe.nop().then_inc(S("gen_free"), GROUP)

                def general_block(b):
                    for w in range(ET // GEN_WIN):
                        above_zero(pe, S("gen_step"), b * (ET // GEN_WIN) + w)
                        count_window(b * ET + w * GEN_WIN, GEN_WIN, 0, S("gen_hot"), S("gen_free"))
                    turn_counts(b)
                general_block(0)
                with pe.Fori(1, T) as b:
                    general_block(b)
            pe.end_ifs()

            def turn_rows(made0, n0):
                for i in range(T):
                    pe.wait_ge(S("xn_made"), made0 + i + 1)
                    above_zero(pe, S("xt_moved"), n0 + i - 1 if i > 1 else n0)
                    for c in range(C):
                        ins = pe.transpose(bank(i % 2, 128, P, c * P), XN[:, i, c * 128:c * 128 + 128],
                                           ident[0:P, 0:P])
                    ins.then_inc(S("xt_turned"), 1)

            pe.wait_ge(S("w_in"), 16)
            pe.wait_ge(S("packed_out"), T)
            turn_rows(0, 0)
            pe.wait_ge(S("xt_moved"), T)
            pe.wait_ge(S("lnct_moved"), 3 * T)
            n = 0
            for part in (1, 0):
                for j in range(4):
                    for q, (a, z) in enumerate(PIECES):
                        above_zero(pe, S("qk_moved"), n - 3)
                        for c in range(C):
                            w = part * D + j * 128
                            ins = pe.matmul(bank(2 + n % 4, 128, z - a), Wqkv[:, c, w:w + 128], XT[:, c, a:z],
                                            start=c == 0, stop=c == C - 1)
                        ins.then_inc(S("qk_made"), 1)
                        n += 1
            for i in range(T):
                above_zero(pe, S("v_moved"), i - 1)
                for c in range(C):
                    ins = pe.matmul(bank(i % 2, P), XT[:, c, i * P:i * P + P], Wqkv[:, c, 2 * D:3 * D],
                                    start=c == 0, stop=c == C - 1)
                ins.then_inc(S("v_turned"), 1)
            pe.wait_ge(S("v_moved"), T)
            pe.wait_ge(S("qk_moved"), 24)

            def scores(u, h, buf, j_staged):
                r = DH * (h % 2)
                pe.wait_ge(S("q_staged"), j_staged)
                above_zero(pe, S("z_made"), u - 1)
                for q, (a, z) in enumerate(PIECES):
                    ins = pe.matmul(bank(3 * buf + q, P, z - a), Qst[r:r + DH, h // 2, :],
                                    KT[r:r + DH, h // 2, a:z], start=True, stop=True)
                ins.then_inc(S("s_made"), 1)

            def head(u, i, h, more, guard):
                buf = h % 2
                pe.wait_ge(S("p_made"), u + 1)
                for q, (a, z) in enumerate(TPIECES):
                    if q == 0 and guard:
                        pe.wait_ge(S("pt_moved_a"), 2 * u)
                    if q == 1 and guard:
                        pe.wait_ge(S("o_moved"), u)
                    if q == 2:
                        pe.wait_ge(S("pt_moved_a"), 2 * u + 1)
                    for jj in range(a, z):
                        ins = pe.transpose(bank(6 + q % 2, P, P, (jj - a) * P), PR[buf][:, jj * P:jj * P + P],
                                           ident[0:P, 0:P])
                    ins.then_inc(S("p_turned"), 1)
                if more:
                    if h < 6:
                        scores(u + 2, h + 2, buf, i * 4 + (h + 2) // 2 + 1)
                    else:
                        scores(u + 2, h - 6, buf, i * 4 + 5)
                pe.wait_ge(S("pt_moved_a"), 2 * u + 2)
                pe.wait_ge(S("pt_moved_v"), u + 1)
                for jj in range(T):
                    ins = pe.matmul(bank(7, P, DH), PT[buf][:, jj, :],
                                    XN[:, jj, h * DH:h * DH + DH], start=jj == 0, stop=jj == T - 1)
                ins.then_inc(S("o_made"), 1)

            scores(0, 0, 0, 1)
            scores(1, 1, 1, 1)
            for h in range(HEADS):
                head(h, 0, h, True, h > 0)
            with pe.Fori(1, T - 1) as i:
                for h in range(HEADS):
                    head(i * HEADS + h, i, h, True, True)
            for h in range(HEADS):
                head((T - 1) * HEADS + h, T - 1, h, h < 6, True)
            pe.wait_ge(S("x_added"), T * HEADS)

            def router(gate_sem, made, n_exp, first):
                pe.wait_ge(gate_sem, 16)
                for i in range(T):
                    for c in range(C):
                        ins = pe.matmul(bank(2, P, n_exp, 8 * i), XT[:, c, i * P:i * P + P],
                                        gate_w[:, c, 0:n_exp], start=c == 0, stop=c == C - 1,
                                        skip_group_check=True)
                ins.then_inc(made, 1)

            def rank(mask_sem, mask_v, m, made):
                pe.wait_ge(mask_sem, mask_v)
                pe.matmul(bank(3, P, 8 * T), before[0:P, 0:P], m, start=True, stop=True)
                pe.matmul(bank(3, 128, 8 * T, 128), ones[0:P, :], m, start=True, stop=True,
                          skip_group_check=True).then_inc(made, 1)

            turn_rows(T, T)
            pe.wait_ge(S("xt_moved"), 2 * T)
            router(S("gate_in"), S("log_made"), E0, True)
            rank(S("mask_made"), 3, mask[:, 2, :, :].rearrange("p i e -> p (i e)"), S("rank_made"))
            pe.wait_ge(S("slot_made"), 1)
            pe.wait_ge(S("w1e_in"), 16 * E0)
            pe.wait_ge(S("w2e_in"), 16 * E0)
            pe.wait_ge(S("w3e_in"), 16 * E0)

            def turn_lane(k, bk, source, n, turned, rows_=TM):
                for c in range(n):
                    ins = pe.transpose(bank(bk, 128, rows_, c * rows_), source[:, c * 128:c * 128 + 128],
                                       ident[0:rows_, 0:rows_])
                ins.then_inc(turned, 1)

            def expert_product(k, bk, lhs, weights, e, n, width, made):
                for c in range(n):
                    ins = pe.matmul(bank(bk, TM, width), lhs[:, c * TM:c * TM + TM],
                                    weights.rearrange("p e n -> p (e n)")[:, bass.ds(e * (n * width) + c * width, width)],
                                    start=c == 0, stop=c == n - 1)
                ins.then_inc(made, 1)

            def mix0(g, guard):
                lanes_ = range(LANES)
                e = [pe.value_load(owner_i[0:1, bass.ds(g * LANES + k, 1)], min_val=0, max_val=E0 - 1)
                     for k in lanes_]
                for k in lanes_:
                    pe.wait_ge(xs_in[k], 16 * g + 16)
                    turn_lane(k, 2 * k, xs[k], C, S("xs_turned"))
                for k in lanes_:
                    pe.wait_ge(S("xs_moved"), g * LANES + k + 1)
                    if guard:
                        pe.wait_ge(S("y_moved"), g * LANES + k + 1 - LANES)
                    expert_product(k, 2 * k + 1, xsT[k], W1E, e[k], C, H0, S("h1_made"))
                for k in lanes_:
                    pe.wait_ge(S("n1_made"), g * LANES + k + 1)
                    turn_lane(k, 2 * k, h1n[k], 2, S("h1_turned"))
                for k in lanes_:
                    pe.wait_ge(S("h1_moved"), g * LANES + k + 1)
                    expert_product(k, 2 * k + 1, hT[k], W2E, e[k], 2, H0, S("h2_made"))
                for k in lanes_:
                    pe.wait_ge(S("n2_made"), g * LANES + k + 1)
                    turn_lane(k, 2 * k, h2n[k], 2, S("h2_turned"))
                for k in lanes_:
                    pe.wait_ge(S("h2_moved"), g * LANES + k + 1)
                    expert_product(k, 2 * k + 1, hT[k], W3E, e[k], 2, D, S("y_made"))
            mix0(0, False)
            with pe.Fori(1, MT0 // LANES) as g:
                mix0(g, True)
            pe.wait_ge(S("y_moved"), MT0)

            pe.wait_ge(S("counts_in"), 16)
            pe.wait_ge(S("hs_made"), T)
            pe.wait_ge(S("wg_in"), 16)

            def project(j):
                b = j % 2
                pe.wait_ge(S("agg_moved"), j + 1)
                above_zero(pe, S("agt_moved"), j - 1)
                for c in range(C):
                    ins = pe.transpose(bank(2 + b, 128, P, c * P), AGG[b][:, c * 128:c * 128 + 128],
                                       ident[0:P, 0:P])
                ins.then_inc(S("agg_turned"), 1)
                pe.wait_ge(S("agt_moved"), j + 1)
                above_zero(pe, S("hg_biased"), j - 1)
                for c in range(C):
                    ins = pe.matmul(bank(4 + b, P), AGT[b][:, c, 0:P], WG[:, c, :], start=c == 0, stop=c == C - 1)
                ins.then_inc(S("hg_made"), 1)
            for j in range(T):
                above_zero(pe, S("agg_moved"), j - 1)
                for i in range(T):
                    ins = pe.matmul(bank(j % 2, P), CS[:, i, j * P:j * P + P], XN[:, i, :],
                                    start=i == 0, stop=i == T - 1)
                ins.then_inc(S("agg_made"), 1)
                if j:
                    project(j - 1)
            project(T - 1)

            turn_rows(2 * T, 2 * T)
            pe.wait_ge(S("xt_moved"), 3 * T)
            pe.wait_ge(S("hg_biased"), T)
            router(S("gate1_in"), S("log1_made"), E1, False)
            rank(S("log1_top"), 1, mask[:, 0, :, :].rearrange("p i e -> p (i e)"), S("rank1_made"))
            pe.wait_ge(S("slot1_made"), 1)
            pe.wait_ge(S("w1b_in"), 16 * E1)
            pe.wait_ge(S("w2b_in"), 16 * E1)

            def mix1(g, guard):
                lanes_ = range(LANES)
                e = [pe.value_load(owner_i[0:1, bass.ds(g * LANES + k, 1)], min_val=0, max_val=E1 - 1)
                     for k in lanes_]
                for k in lanes_:
                    pe.wait_ge(z_in[k], 16 * g + 16)
                    turn_lane(k, 2 * k, xs[k], C, S("z_turned"))
                for k in lanes_:
                    pe.wait_ge(S("z_moved"), g * LANES + k + 1)
                    if guard:
                        pe.wait_ge(S("yy_moved"), g * LANES + k + 1 - LANES)
                    expert_product(k, 2 * k + 1, xsT[k], W1B, e[k], C, H1, S("hh_made"))
                for k in lanes_:
                    pe.wait_ge(S("gg_made"), g * LANES + k + 1)
                    turn_lane(k, 2 * k, act1[k], 2, S("gg_turned"))
                for k in lanes_:
                    pe.wait_ge(S("gg_moved"), g * LANES + k + 1)
                    expert_product(k, 2 * k + 1, hT[k], W2B, e[k], 2, D, S("yy_made"))
            mix1(0, False)
            with pe.Fori(1, MT1 // LANES) as g:
                mix1(g, True)

        @block.scalar
        def _(act):
            act.wait_ge(S("ctl_ready"), 1)
            all_hold = act.value_load(ctl[0:1, T:T + 1], min_val=0, max_val=1)

            def move_packed(b, buf):
                act.wait_ge(S("slots_free"), b * WIN + (WIN + GROUP))
                above_zero(act, S("unpacked_out"), b)
                act.activation(packed, ps[0:P, 1024 * buf:1024 * buf + HALF], ACT.Copy)\
                   .then_inc(S("packed_out"), 1)

            def counts_and_logs(b):
                act.wait_ge(S("unpacked_out"), b + 1)
                above_zero(act, S("lnct_turned"), 3 * b)
                act.activation(CT, unpacked, ACT.Copy, accum_out=deg_in[:, bass.ds(b, 1)])\
                   .then_inc(S("ct_made"), 1)
                act.wait_ge(S("max_made"), b + 1)
                act.activation(lnCT, lnCT, ACT.Ln).then_inc(S("ln_made"), 1)
                above_zero(act, S("counts_out"), b * 16)
                for q, (a, z) in enumerate(TPIECES):
                    act.wait_ge(S("ct_turned"), 3 * b + q + 1)
                    act.activation(stage[:, a:z, :],
                                   bank(4 + q, P, (z - a) * P).rearrange("p (i n) -> p i n", n=P), ACT.Copy)\
                       .then_inc(S("ct_moved"), 1)
                above_zero(act, S("logs_out"), b * 16)
                for q, (a, z) in enumerate(TPIECES):
                    act.wait_ge(S("lnct_turned"), 3 * b + q + 1)
                    act.activation(ln_stage[:, a:z, :],
                                   bank(4 + q, P, (z - a) * P).rearrange("p (i n) -> p i n", n=P), ACT.Copy)\
                       .then_inc(S("lnct_moved"), 1)

            with act.If(all_hold):
                move_packed(0, 0)
                counts_and_logs(0)
                move_packed(1, 1)
                with act.Fori(2, T, 2) as b:
                    counts_and_logs(b - 1)
                    move_packed(b, 0)
                    counts_and_logs(b)
                    move_packed(b + 1, 1)
                counts_and_logs(T - 1)
            with act.Else():
                counts_and_logs(0)
                with act.Fori(1, T) as b:
                    counts_and_logs(b)
                act.wait_ge(S("gen_free"), T * ET + GROUP)
                act.nop().then_inc(S("packed_out"), T)
            act.end_ifs()

            def move_rows(n0):
                for i in range(T):
                    act.wait_ge(S("xt_turned"), n0 + i + 1)
                    act.activation(XT[:, :, i * P:i * P + P],
                                   bank(i % 2, 128, C * P).rearrange("p (c n) -> p c n", c=C), ACT.Copy)\
                       .then_inc(S("xt_moved"), 1)
            move_rows(0)
            act.wait_ge(S("zeros_out"), 32)
            n = 0
            for part in (1, 0):
                for j in range(4):
                    for q, (a, z) in enumerate(PIECES):
                        act.wait_ge(S("qk_made"), n + 1)
                        act.activation((KT if part else QT)[:, j, a:z], bank(2 + n % 4, 128, z - a), ACT.Copy,
                                       scale=1.0 if part else DH ** -0.5).then_inc(S("qk_moved"), 1)
                        n += 1

            def exponential(u, h, guard):
                buf = h % 2
                act.wait_ge(S("z_made"), u + 1)
                if guard:
                    act.wait_ge(S("p_turned"), 3 * u - 3)
                act.activation(PR[buf], SC[buf], ACT.Exp, bias=neg_max[:, h % 4:h % 4 + 1], scale=-1.0,
                               accum_out=den[:, buf:buf + 1]).then_inc(S("p_made"), 1)

            def move_turned(u, h):
                buf = h % 2
                for q in (0, 2):
                    a, z = TPIECES[q]
                    act.wait_ge(S("p_turned"), 3 * u + q + 1)
                    if q == 0:
                        above_zero(act, S("o_made"), u - 1)
                    act.activation(PT[buf][:, a:z, :],
                                   bank(6 + q % 2, P, (z - a) * P).rearrange("p (i n) -> p i n", n=P), ACT.Copy)\
                       .then_inc(S("pt_moved_a"), 1)

            def move_output(u, h):
                act.wait_ge(S("o_made"), u + 1)
                act.wait_ge(S("rden_made"), 2 * u + 2)
                above_zero(act, S("x_added"), u - 1)
                act.activation(head_out[:, h % 2, :], bank(7, P, DH), ACT.Copy, scale=rden[:, h % 2:h % 2 + 1])\
                   .then_inc(S("o_moved"), 1)
            exponential(0, 0, False)
            for h in range(HEADS):
                move_turned(h, h)
                exponential(h + 1, h + 1, h >= 1)
                move_output(h, h)
            with act.Fori(1, T - 1) as i:
                for h in range(HEADS):
                    move_turned(i * HEADS + h, h)
                    exponential(i * HEADS + h + 1, h + 1, True)
                    move_output(i * HEADS + h, h)
            for h in range(HEADS):
                move_turned((T - 1) * HEADS + h, h)
                if h < HEADS - 1:
                    exponential((T - 1) * HEADS + h + 1, h + 1, True)
                move_output((T - 1) * HEADS + h, h)

            move_rows(T)
            act.wait_ge(S("gate_step"), 1)
            act.activation(gates[:, 0, :], gates[:, 0, :], ACT.Exp).then_inc(S("gate_exp"), 1)

            def mix0(g):
                lanes_ = range(LANES)
                for k in lanes_:
                    act.wait_ge(S("xs_turned"), g * LANES + k + 1)
                    act.activation(xsT[k], bank(2 * k), ACT.Copy).then_inc(S("xs_moved"), 1)
                for k in lanes_:
                    act.wait_ge(S("h1_made"), g * LANES + k + 1)
                    act.activation(act1[k], bank(2 * k + 1, TM, H0), ACT.Gelu).then_inc(S("g1_made"), 1)
                for k in lanes_:
                    act.wait_ge(S("h1_turned"), g * LANES + k + 1)
                    act.activation(hT[k], bank(2 * k, 128, 256), ACT.Copy).then_inc(S("h1_moved"), 1)
                for k in lanes_:
                    act.wait_ge(S("h2_made"), g * LANES + k + 1)
                    act.activation(act1[k], bank(2 * k + 1, TM, H0), ACT.Gelu).then_inc(S("g2_made"), 1)
                for k in lanes_:
                    act.wait_ge(S("h2_turned"), g * LANES + k + 1)
                    act.activation(hT[k], bank(2 * k, 128, 256), ACT.Copy).then_inc(S("h2_moved"), 1)
            with act.Fori(0, MT0 // LANES) as g:
                mix0(g)

            for j in range(T):
                b = j % 2
                act.wait_ge(S("agg_turned"), j + 1)
                act.activation(AGT[b][:, :, 0:P],
                               bank(2 + b, 128, C * P).rearrange("p (c n) -> p c n", c=C), ACT.Copy)\
                   .then_inc(S("agt_moved"), 1)
                if j:
                    act.wait_ge(S("hg_shift"), j)
                    act.activation(HG[1 - b], HG[1 - b], ACT.Gelu).then_inc(S("hg_gelu"), 1)
            act.wait_ge(S("hg_shift"), T)
            act.activation(HG[1], HG[1], ACT.Gelu).then_inc(S("hg_gelu"), 1)

            move_rows(2 * T)
            act.wait_ge(S("g1_step"), 3)
            act.activation(logits[:, :, 0:E1], logits[:, :, 0:E1], ACT.Exp).then_inc(S("g1_exp"), 1)

            def mix1(g):
                lanes_ = range(LANES)
                for k in lanes_:
                    act.wait_ge(S("z_turned"), g * LANES + k + 1)
                    act.activation(xsT[k], bank(2 * k), ACT.Copy).then_inc(S("z_moved"), 1)
                for k in lanes_:
                    act.wait_ge(S("hh_made"), g * LANES + k + 1)
                    act.activation(act1[k], bank(2 * k + 1, TM, H1), ACT.Gelu).then_inc(S("gg_made"), 1)
                for k in lanes_:
                    act.wait_ge(S("gg_turned"), g * LANES + k + 1)
                    act.activation(hT[k], bank(2 * k, 128, 256), ACT.Copy).then_inc(S("gg_moved"), 1)
            with act.Fori(0, MT1 // LANES) as g:
                mix1(g)

        @block.gpsimd
        def _(pool):
            c = [0]

            def link(ins):
                c[0] += 1
                ins.then_inc(S("chain"), 1)
                pool.wait_ge(S("chain"), c[0])
            pool.memset(zero_rows, 0.0).then_inc(S("zero_made"), 1)
            pool.memset(ident[:, :], 0.0)
            pool.memset(ones[:, :], 1.0)
            pool.memset(half_pow[:, :], -0.5)
            link(pool.iota(tile_off[:, :], [[P, T]], base=0, channel_multiplier=0,
                           allow_small_or_imprecise_dtypes=True))
            pool.iota(iota_src, [[1, HALF]], base=0, channel_multiplier=0)
            pool.iota(iota_dst, [[1, P]], base=0, channel_multiplier=0)
            pool.iota(iota8[:, :], [[1, 8]], base=0, channel_multiplier=0, allow_small_or_imprecise_dtypes=True)
            pool.iota(iotaT[:, :], [[1, MT0]], base=0, channel_multiplier=0, allow_small_or_imprecise_dtypes=True)
            pool.iota(span_tmp[:, 0, :], [[1, 2], [2, 80]], base=0, channel_multiplier=0,
                      allow_small_or_imprecise_dtypes=True)
            pool.iota(span_tmp[:, 1, :], [[1, 2], [2, 80]], base=int(BIG), channel_multiplier=0,
                      allow_small_or_imprecise_dtypes=True)
            link(pool.iota(spans[:, 0:2], [[P, 2]], base=0, channel_multiplier=P,
                           allow_small_or_imprecise_dtypes=True))
            pool.affine_select(out=before[:, :], in_=ones[:, :], compare_op=ALU.is_gt, fill=0.0, base=0,
                               pattern=[[1, 128]], channel_multiplier=-1)
            pool.affine_select(out=ident[:, :], in_=ident[:, :], compare_op=ALU.not_equal, fill=1.0, base=0,
                               pattern=[[-1, 128]], channel_multiplier=1).then_inc(S("consts"), 1)

            def rstd_all(waited, n, eps, made):
                pool.wait_ge(waited, n)
                link(pool.tensor_scalar(rstd[0:P, :], mv[0:P, :, 1], 1.0, eps, ALU.mult, ALU.add))
                pool.tensor_tensor(rstd[0:P, :], rstd[0:P, :], half_pow[0:P, :], ALU.pow).then_inc(made, 1)
            rstd_all(S("ln_stat"), T, LN_EPS, S("ln_rstd"))

            pool.wait_ge(S("qk_moved"), 24)
            for j in range(4):
                pool.tensor_copy(Qst[:, j, :], QT[:, j, 0:P]).then_inc(S("q_staged"), 1)

            def add_heads(i, stage_next):
                for h in range(HEADS):
                    if stage_next and h % 2 == 0:
                        j = h // 2
                        pool.wait_ge(S("s_made"), i * HEADS + h + 2)
                        pool.tensor_copy(Qst[:, j, :], QT[:, j, bass.ds(i * P + P, P)]).then_inc(S("q_staged"), 1)
                    xa = X[:, :, :].rearrange("p i d -> p (i d)")[:, bass.ds(i * D + h * DH, DH)]
                    pool.wait_ge(S("o_moved"), i * HEADS + h + 1)
                    pool.tensor_tensor(xa, xa, head_out[:, h % 2, :], ALU.add).then_inc(S("x_added"), 1)
            with pool.Fori(0, T - 1) as i:
                add_heads(i, True)
            add_heads(T - 1, False)

            rstd_all(S("ln_stat"), 2 * T, LN_EPS, S("ln_rstd"))
            pool.wait_ge(S("slot_made"), 1)
            pool.wait_ge(S("zeros_out"), 32)
            pool.wait_ge(S("xn_made"), 2 * T)
            for k in range(K0):
                for i in range(T):
                    pool.indirect_dma_start(slots0_d, bass.IndirectOffsetOnAxis(ap=slot[:, k, i:i + 1], axis=0),
                                            XN[:, i, :], None).then_inc(S("rows_out"), 16)

            def inverse_rms(n, step, made, k):
                pool.wait_ge(step, n)
                pool.tensor_tensor(rms[:, k:k + 1], ssum[:, k:k + 1], half_pow[:, 0:1], ALU.pow).then_inc(made, 1)
            with pool.Fori(0, MT0 // LANES) as g:
                for k in range(LANES):
                    inverse_rms(g * LANES + k + 1, S("rms_step"), S("rms_made"), k)
                for k in range(LANES):
                    inverse_rms(g * LANES + k + 1, S("rms2_step"), S("rms2_made"), k)
            for k in range(LANES):
                pool.wait_ge(y_out[k], 16 * (MT0 // LANES))
            pool.wait_ge(S("y_made"), MT0)
            n = 0
            for i in range(T):
                for k in range(K0):
                    if n >= 8:
                        pool.wait_ge(S("dchain"), n - 7)
                    pool.indirect_dma_start(rows[n % 8], None, made0_d,
                                            bass.IndirectOffsetOnAxis(ap=slot[:, k, i:i + 1], axis=0))\
                        .then_inc(rows_in[n % 8], 16)
                    n += 1

            rstd_all(S("ln_stat"), 3 * T, LN_EPS, S("ln_rstd"))
            pool.wait_ge(S("rank1_step"), 1)
            link(pool.tensor_scalar(inv_in[:, :], deg_in[:, :], 1.0, None, ALU.max))
            link(pool.tensor_scalar(inv_out[:, :], deg_out[:, :], 1.0, None, ALU.max))
            pool.tensor_tensor(inv_in[:, :], inv_in[:, :], half_pow[0:P, :], ALU.pow)
            pool.tensor_tensor(inv_out[:, :], inv_out[:, :], half_pow[0:P, :], ALU.pow).then_inc(S("degi_made"), 1)
            for j in range(T):
                pool.wait_ge(S("hg_stat"), j + 1)
                pool.tensor_scalar(rstd[0:P, j:j + 1], mv[0:P, j, 1:2], 1.0, LN_EPS, ALU.mult, ALU.add)\
                    .then_inc(S("hg_pow"), 1)
                pool.wait_ge(S("hg_pow"), j + 1)
                pool.tensor_tensor(rstd[0:P, j:j + 1], rstd[0:P, j:j + 1], half_pow[0:P, 0:1], ALU.pow)\
                    .then_inc(S("hg_rstd"), 1)
            for n in (4 * T, 5 * T):
                rstd_all(S("ln_stat"), n, LN_EPS, S("ln_rstd"))
            pool.wait_ge(S("slot1_made"), 1)
            pool.wait_ge(S("xn_made"), 4 * T)
            for i in range(T):
                pool.indirect_dma_start(slots1_d, bass.IndirectOffsetOnAxis(ap=slot[:, 0, i:i + 1], axis=0),
                                        XN[:, i, :], None).then_inc(S("rows1_out"), 16)
            for k in range(LANES):
                pool.wait_ge(yy_out[k], 16 * (MT1 // LANES))
            pool.wait_ge(S("yy_made"), MT1)
            for i in range(T):
                n = K0 * T + i
                if i >= 8:
                    pool.wait_ge(S("dchain"), K0 * T + i - 7)
                pool.indirect_dma_start(rows[i % 8], None, made1_d,
                                        bass.IndirectOffsetOnAxis(ap=slot[:, 0, i:i + 1], axis=0))\
                    .then_inc(rows_in[i % 8], 16)

        @block.vector
        def _(dve):
            c = [0]

            def link(ins):
                c[0] += 1
                ins.then_inc(S("degs_made"), 1)
                dve.wait_ge(S("degs_made"), c[0])

            dve.wait_ge(S("edges_in"), 32)
            dve.tensor_copy(idx_f[:, 0, :], raw_idx[:, 0, :]).then_inc(S("idx_step"), 1)
            dve.tensor_copy(src_f, raw_idx[:, 1, :]).then_inc(S("idx_step"), 1)
            dve.wait_ge(S("idx_step"), 2)
            dve.tensor_scalar(upper, src_f, float(HALF), None, ALU.is_ge).then_inc(S("idx_step"), 1)
            dve.wait_ge(S("idx_step"), 3)
            dve.scalar_tensor_tensor(idx_f[:, 1, :], upper, -float(HALF), src_f, ALU.mult, ALU.add)\
               .then_inc(S("idx_step"), 1)
            dve.tensor_scalar(idx_f[:, 2, :], upper, float(2 ** SHIFT - 1), 1.0, ALU.mult, ALU.add)\
               .then_inc(S("idx_step"), 1)
            for k, op in ((0, ALU.min), (2, ALU.max)):
                ins = dve.tensor_reduce(bounds[:, k:k + 2],
                                        idx_f[:, 0, :].rearrange("p (r e) -> p r e", r=2), X_AXIS, op)
                link(ins)
            dve.wait_ge(S("consts"), 1)
            for k in range(4):
                dve.tensor_scalar(span_diag[:, k, :], ident[0:80, 0:80], bounds[:, k:k + 1], None, ALU.mult)\
                   .then_inc(S("diag_made"), 1)
            dve.wait_ge(S("idx_turned"), 1)
            link(dve.tensor_copy(idxT.rearrange("p k (q r) -> p k r q", r=2),
                                 bank(6, EP, 480).rearrange("p (k r q) -> p k r q", k=3, r=2)))
            dve.wait_ge(S("span_sums"), 1)
            least, greatest = bank(7, T, ET), bank(7, T, ET, ET)
            def step(ins, n):
                ins.then_inc(S("span_step"), 1)
                dve.wait_ge(S("span_step"), n)
            step(dve.tensor_scalar(span_tmp[:, 2, :], least, spans[:, 1:2], None, ALU.is_lt), 1)
            step(dve.scalar_tensor_tensor(span_tmp[:, 2, :], greatest, spans[:, 0:1], span_tmp[:, 2, :],
                                          ALU.is_ge, ALU.mult), 2)
            step(dve.scalar_tensor_tensor(span_tmp[:, 3, :], span_tmp[:, 2, :], -BIG, span_tmp[:, 1, :],
                                          ALU.mult, ALU.add), 3)
            dve.tensor_tensor(span_tmp[:, 4, :], span_tmp[:, 2, :], span_tmp[:, 0, :], ALU.mult)
            step(dve.tensor_reduce(spans[:, 2:3], span_tmp[:, 3, :], X_AXIS, ALU.min), 4)
            step(dve.tensor_reduce(spans[:, 3:4], span_tmp[:, 4, :], X_AXIS, ALU.max), 5)
            step(dve.tensor_tensor(spans[:, 4:5], spans[:, 3:4], spans[:, 2:3], ALU.subtract), 6)
            step(dve.tensor_scalar(spans[:, 6:7], spans[:, 2:3], float(ET - WIN), 0.0, ALU.min, ALU.max), 7)
            step(dve.tensor_scalar(spans[:, 7:8], spans[:, 4:5], float(WIN - 1), None, ALU.is_le), 8)
            dve.wait_ge(S("ctl_sums"), 1)
            link(dve.tensor_copy(ctl_f[:, 0:T], bank(7, 1, T, 320)))
            link(dve.tensor_reduce(ctl_f[:, T:T + 1], bank(7, 1, T, 336), X_AXIS, ALU.min))
            dve.tensor_copy(ctl[:, 0:T + 1], ctl_f[:, 0:T + 1]).then_inc(S("ctl_ready"), 1)

            def layer_norm_stats(source, ready=None):
                for i in range(T):
                    if ready is not None:
                        ready(i)
                    link(dve.bn_stats(stats[0:P, i, :], source[:, i, :]))
                    dve.bn_aggr(mv[0:P, i, :], stats[0:P, i, :]).then_inc(S("ln_stat"), 1)

            def layer_norm_rows(n, source, scale=None):
                dve.wait_ge(S("ln_rstd"), n)
                for i in range(T):
                    if scale is None:
                        dve.tensor_scalar(XN[:, i, :], source[:, i, :], mv[0:P, i, 0:1], rstd[0:P, i:i + 1],
                                          ALU.subtract, ALU.mult).then_inc(S("xn_made"), 1)
                    else:
                        link(dve.tensor_scalar(XN[:, i, :], source[:, i, :], mv[0:P, i, 0:1], rstd[0:P, i:i + 1],
                                               ALU.subtract, ALU.mult))
                        scale(i)
            dve.wait_ge(S("x_in"), 16)
            layer_norm_stats(X)
            layer_norm_rows(1, X)

            dve.wait_ge(S("ctl_ready"), 1)
            all_hold = dve.value_load(ctl[0:1, T:T + 1], min_val=0, max_val=1)

            def unpack(b, source_sem, source_n):
                dve.wait_ge(source_sem, source_n)
                above_zero(dve, S("ct_made"), b)
                dve.tensor_scalar(unpacked[:, 0:HALF], packed, 2 ** SHIFT - 1, None, ALU.bitwise_and)
                dve.tensor_scalar(unpacked[:, HALF:N], packed, SHIFT, None, ALU.logical_shift_right)\
                   .then_inc(S("unpacked_out"), 1)

            def floor_one(b):
                dve.wait_ge(S("ct_made"), b + 1)
                dve.tensor_scalar(lnCT, CT, 1.0, None, ALU.max).then_inc(S("max_made"), 1)
                dve.tensor_scalar(penalty, CT, 0.5, NEG, ALU.is_lt, ALU.mult).then_inc(S("pen_made"), 1)

            def log_counts(b):
                dve.wait_ge(S("ln_made"), b + 1)
                dve.wait_ge(S("pen_made"), b + 1)
                dve.tensor_tensor(lnCT, lnCT, penalty, ALU.add).then_inc(S("lnct_made"), 1)

            def hot_group(g0, w0, hot, free):
                for k in range(GROUP):
                    dve.wait_ge(free, g0 + k + 1)
                    dve.tensor_scalar(oh_dst[:, k, :], iota_dst, win[:, 0, w0 + k:w0 + k + 1], None, ALU.is_equal)
                    dve.tensor_scalar(oh_src[:, k, :], iota_src, win[:, 1, w0 + k:w0 + k + 1],
                                      win[:, 2, w0 + k:w0 + k + 1], ALU.is_equal, ALU.mult).then_inc(hot, 1)

            def make_window(b, start, tiles, made, n):
                off = tile_off[0:EP, bass.ds(b, 1)] if not isinstance(b, int) else tile_off[0:EP, b:b + 1]
                dve.tensor_scalar(win[:, 0, 0:tiles], idxT[:, 0, bass.ds(start, tiles)], off, None, ALU.subtract)
                dve.tensor_copy(win[:, 1:3, 0:tiles], idxT[:, 1:3, bass.ds(start, tiles)]).then_inc(made, 1)
                dve.wait_ge(made, n)

            def fast_block(b, after):
                start = dve.value_load(ctl[0:1, bass.ds(b, 1)], min_val=0, max_val=ET - WIN)
                above_zero(dve, S("hot"), b * WIN)
                make_window(b, start, WIN, S("win_made"), b + 1)
                for w0 in range(0, WIN, GROUP):
                    hot_group(b * WIN + w0, w0, S("hot"), S("slots_free"))
                    if after is not None and w0 == 0:
                        unpack(after, S("packed_out"), after + 1)
                    if after is not None and w0 == 8:
                        floor_one(after)
                    if after is not None and w0 == 16:
                        log_counts(after)
            with dve.If(all_hold):
                fast_block(0, None)
                fast_block(1, 0)
                with dve.Fori(2, T) as b:
                    fast_block(b, b - 1)
                unpack(T - 1, S("packed_out"), T)
                floor_one(T - 1)
                log_counts(T - 1)
            with dve.Else():
                NW = ET // GEN_WIN
                with dve.Fori(0, T) as b:
                    for w in range(NW):
                        if w:
                            dve.wait_ge(S("gen_hot"), b * ET + w * GEN_WIN)
                        make_window(b, w * GEN_WIN, GEN_WIN, S("gen_win"), b * NW + w + 1)
                        for w0 in range(0, GEN_WIN, GROUP):
                            hot_group(b * ET + w * GEN_WIN + w0, w0, S("gen_hot"), S("gen_free"))
                        dve.wait_ge(S("gen_free"), b * ET + w * GEN_WIN + (GEN_WIN + GROUP))
                        gs = b * (4 * NW) + 4 * w
                        def gstep(ins, n):
                            ins.then_inc(S("rank_step"), 1)
                            dve.wait_ge(S("rank_step"), gs + n)
                        gstep(dve.tensor_copy(packed, ps[0:P, 0:HALF]), 1)
                        gstep(dve.tensor_scalar(unpacked[:, 0:HALF], packed, 2 ** SHIFT - 1, None, ALU.bitwise_and), 2)
                        gstep(dve.tensor_scalar(unpacked[:, HALF:N], packed, SHIFT, None, ALU.logical_shift_right), 3)
                        if w == 0:
                            dve.tensor_copy(sumCT, unpacked).then_inc(S("rank_step"), 1)
                        else:
                            dve.tensor_tensor(sumCT, sumCT, unpacked, ALU.add).then_inc(S("rank_step"), 1)
                        dve.wait_ge(S("rank_step"), gs + 4)
                        if w < NW - 1:
                            dve.nop().then_inc(S("gen_step"), 1)
                    dve.tensor_copy(unpacked, sumCT).then_inc(S("unpacked_out"), 1)
                    dve.nop().then_inc(S("gen_step"), 1)
                    floor_one(b)
                    log_counts(b)
                    dve.wait_ge(S("lnct_turned"), 3 * b + 3)
            dve.end_ifs()

            for i in range(T):
                dve.wait_ge(S("v_turned"), i + 1)
                if i == 0:
                    dve.wait_ge(S("xt_turned"), T)
                dve.tensor_copy(XN[:, i, :], bank(i % 2, P)).then_inc(S("v_moved"), 1)
            dve.wait_ge(S("lnct_moved"), 3 * T)

            def await_scores(u, tb, nth_logs, h):
                if h == 0:
                    dve.wait_ge(logs_in[tb], nth_logs)
                dve.wait_ge(S("s_made"), u + 1)
                above_zero(dve, S("p_made"), u - 1)

            def negate_scores(tb, h):
                buf = h % 2
                dve.tensor_tensor_reduce(SC[buf], ps[0:P, 1536 * buf:1536 * buf + N], LNB[tb],
                                         -1.0, 3.0e38, ALU.add, ALU.min, neg_max[:, h % 4:h % 4 + 1]).then_inc(S("z_made"), 1)

            def move_turned(u, h):
                buf = h % 2
                a, z = TPIECES[1]
                dve.wait_ge(S("p_turned"), 3 * u + 2)
                above_zero(dve, S("o_made"), u - 1)
                dve.tensor_copy(PT[buf][:, a:z, :], bank(7, P, (z - a) * P).rearrange("p (i n) -> p i n", n=P))\
                   .then_inc(S("pt_moved_v"), 1)

            def inverse_den(u, i, h):
                buf = h % 2
                dve.wait_ge(S("p_made"), u + 1)
                above_zero(dve, S("o_moved"), u - 1)
                dve.reciprocal(rden[:, buf:buf + 1], den[:, buf:buf + 1]).then_inc(S("rden_made"), 1)
                dve.wait_ge(S("rden_made"), 2 * u + 1)
                dve.scalar_tensor_tensor(rden[:, buf:buf + 1], neg_max[:, h % 4:h % 4 + 1], -0.1 * NEG,
                                         rden[:, buf:buf + 1], ALU.is_lt, ALU.mult).then_inc(S("rden_made"), 1)

            def attend(i, tb, nth_logs, last=False):
                for h in range(HEADS):
                    u = i * HEADS + h
                    more = not (last and h >= HEADS - 2)
                    nxt = (tb, nth_logs, h + 2) if h < HEADS - 2 else (1 - tb, nth_logs + 16 * tb, h + 2 - HEADS)
                    move_turned(u, h)
                    if more:
                        await_scores(u + 2, *nxt)
                    inverse_den(u, i, h)
                    if more:
                        negate_scores(nxt[0], nxt[2])
            dve.wait_ge(S("counts_out"), 16 * T)
            await_scores(0, 0, 16, 0)
            negate_scores(0, 0)
            await_scores(1, 0, 16, 1)
            negate_scores(0, 1)
            attend(0, 0, 16)
            attend(1, 1, 16)
            with dve.Fori(1, T // 2 - 1) as ii:
                attend(2 * ii, 0, 16 * ii + 16)
                attend(2 * ii + 1, 1, 16 * ii + 16)
            attend(T - 2, 0, 8 * T)
            attend(T - 1, 1, 8 * T, last=True)
            dve.wait_ge(S("x_added"), T * HEADS)

            layer_norm_stats(X)
            layer_norm_rows(2, X)
            dve.wait_ge(S("log_made"), 1)
            link(dve.tensor_copy(logits[:, :, :], bank(2, P, 8 * T).rearrange("p (i e) -> p i e", e=8)))
            for i in range(T):
                link(dve.max(top[:, i, :], logits[:, i, :]))
                link(dve.max_index(top_i[:, i, :], top[:, i, :], logits[:, i, :]))
            link(dve.tensor_copy(pick[:, :, :], top_i[:, :, 0:2]))
            dve.tensor_tensor(gates[:, 0, :], top[:, :, 1], top[:, :, 0], ALU.subtract).then_inc(S("gate_step"), 1)
            iota_b = iota8[:, :].unsqueeze(1).to_broadcast([P, T, 8])
            for k in range(K0):
                dve.tensor_tensor(mask[:, k, :, :], iota_b, pick[:, :, k:k + 1].to_broadcast([P, T, 8]),
                                  ALU.is_equal).then_inc(S("mask_made"), 1)
            dve.wait_ge(S("mask_made"), 2)
            dve.tensor_tensor(mask[:, 2, :, :], mask[:, 0, :, :], mask[:, 1, :, :], ALU.add)\
               .then_inc(S("mask_made"), 1)
            dve.wait_ge(S("gate_exp"), 1)
            link(dve.tensor_scalar(gates[:, 1, :], gates[:, 0, :], 1.0, None, ALU.add))
            link(dve.reciprocal(gates[:, 2, :], gates[:, 1, :]))
            link(dve.tensor_tensor(gates[:, 3, :], gates[:, 0, :], gates[:, 2, :], ALU.mult))

            def slots_of(masks, tiles, experts, made):
                tot = bank(3, 128, 8 * T, 128).rearrange("p (i e) -> p i e", e=8)
                link(dve.memset(place[:, 0, :], 0.0))
                for i in range(1, T):
                    link(dve.tensor_tensor(place[:, i, :], place[:, i - 1, :], tot[:, i - 1, :], ALU.add))
                link(dve.tensor_tensor(cnt[:, 0, :], place[:, T - 1, :], tot[:, T - 1, :], ALU.add))
                link(dve.tensor_scalar(cnt_i[:, :], cnt[:, 0, :], float(TM - 1), None, ALU.add))
                link(dve.tensor_scalar(cnt_i[:, :], cnt_i[:, :], 7, None, ALU.logical_shift_right))
                link(dve.tensor_copy(cnt[:, 1, :], cnt_i[:, :]))
                link(dve.memset(cnt[:, 4, :], 1.0))
                link(dve.tensor_tensor_scan(cnt[:, 2, :], cnt[:, 4, :], cnt[:, 1, :], 0.0, ALU.mult, ALU.add))
                link(dve.tensor_tensor(cnt[:, 3, :], cnt[:, 2, :], cnt[:, 1, :], ALU.subtract))
                link(dve.tensor_scalar(cnt[:, 3, :], cnt[:, 3, :], float(TM), None, ALU.mult))
                link(dve.tensor_tensor(place[0:P, :, :], place[0:P, :, :],
                                       bank(3, P, 8 * T).rearrange("p (i e) -> p i e", e=8), ALU.add))
                link(dve.tensor_tensor(place[0:P, :, :], place[0:P, :, :],
                                       cnt[0:P, 3:4, :].to_broadcast([P, T, 8]), ALU.add))
                for k, m in enumerate(masks):
                    link(dve.tensor_tensor(logits[:, :, :], m, place[0:P, :, :], ALU.mult))
                    link(dve.tensor_reduce(slot_f[:, k, :], logits[:, :, :], X_AXIS, ALU.add))
                    link(dve.tensor_copy(slot[:, k, :], slot_f[:, k, :]))
                link(dve.tensor_tensor(owner[:, 0:tiles, :], iotaT[:, 0:tiles].unsqueeze(2).to_broadcast([1, tiles, 8]),
                                       cnt[0:1, 2:3, :].to_broadcast([1, tiles, 8]), ALU.is_ge))
                link(dve.tensor_reduce(owner_f[:, 0:tiles], owner[:, 0:tiles, :], X_AXIS, ALU.add))
                link(dve.tensor_scalar(owner_f[:, 0:tiles], owner_f[:, 0:tiles], float(experts - 1), None, ALU.min))
                dve.tensor_copy(owner_i[:, 0:tiles], owner_f[:, 0:tiles]).then_inc(made, 1)
                dve.wait_ge(made, 1)
            dve.wait_ge(S("rank_made"), 1)
            slots_of([mask[:, 0, :, :], mask[:, 1, :, :]], MT0, E0, S("slot_made"))
            dve.wait_ge(S("nrm_in"), 32)

            def mix0(g):
                lanes_ = range(LANES)
                e = [dve.value_load(owner_i[0:1, bass.ds(g * LANES + k, 1)], min_val=0, max_val=E0 - 1)
                     for k in lanes_]
                for k in lanes_:
                    n = g * LANES + k + 1
                    dve.wait_ge(S("g1_made"), n)
                    dve.tensor_tensor_reduce(sq[k], act1[k], act1[k], 1.0, 0.0, ALU.mult, ALU.add,
                                             ssum[:, k:k + 1]).then_inc(S("ss_made"), 1)
                    dve.wait_ge(S("ss_made"), n)
                    dve.tensor_scalar(ssum[:, k:k + 1], ssum[:, k:k + 1], 1.0 / H0, RMS_EPS, ALU.mult, ALU.add)\
                       .then_inc(S("rms_step"), 1)
                for k in lanes_:
                    n = g * LANES + k + 1
                    dve.wait_ge(S("rms_made"), n)
                    dve.scalar_tensor_tensor(h1n[k], act1[k], rms[:, k:k + 1], N1B[:, bass.ds(e[k] * H0, H0)],
                                             ALU.mult, ALU.mult).then_inc(S("n1_made"), 1)
                for k in lanes_:
                    n = g * LANES + k + 1
                    dve.wait_ge(S("g2_made"), n)
                    dve.tensor_tensor_reduce(sq[k], act1[k], act1[k], 1.0, 0.0, ALU.mult, ALU.add,
                                             ssum[:, k:k + 1]).then_inc(S("ss2_made"), 1)
                    dve.wait_ge(S("ss2_made"), n)
                    dve.tensor_scalar(ssum[:, k:k + 1], ssum[:, k:k + 1], 1.0 / H0, RMS_EPS, ALU.mult, ALU.add)\
                       .then_inc(S("rms2_step"), 1)
                for k in lanes_:
                    n = g * LANES + k + 1
                    dve.wait_ge(S("rms2_made"), n)
                    dve.scalar_tensor_tensor(h2n[k], act1[k], rms[:, k:k + 1], N2B[:, bass.ds(e[k] * H0, H0)],
                                             ALU.mult, ALU.mult).then_inc(S("h2_scaled"), 1)
                    dve.wait_ge(S("h2_scaled"), n)
                    dve.tensor_tensor(h2n[k], h2n[k], h1n[k], ALU.add).then_inc(S("n2_made"), 1)
                for k in lanes_:
                    n = g * LANES + k + 1
                    dve.wait_ge(S("y_made"), n)
                    above_zero(dve, y_out[k], g * 16)
                    dve.tensor_copy(ys[k], bank(2 * k + 1)).then_inc(S("y_moved"), 1)
            mix0(0)
            with dve.Fori(1, MT0 // LANES) as g:
                mix0(g)

            def add_rows(n, i, gate):
                dve.wait_ge(rows_in[n % 8 if n < K0 * T else i % 8],
                            16 * (n // 8 + 1) if n < K0 * T else 16 * (len(range(i % 8, K0 * T, 8)) + i // 8 + 1))
                dve.scalar_tensor_tensor(X[:, i, :], rows[n % 8 if n < K0 * T else i % 8], gate, X[:, i, :],
                                         ALU.mult, ALU.add).then_inc(S("dchain"), 1)
                dve.wait_ge(S("dchain"), n + 1)
            for i in range(T):
                for k in range(K0):
                    add_rows(K0 * i + k, i, gates[:, 2 + k, i:i + 1])

            layer_norm_stats(X)
            dve.wait_ge(S("counts_in"), 16)
            for i in range(T):
                link(dve.tensor_reduce(deg_out[:, i:i + 1], CS[:, i, :], X_AXIS, ALU.add))
            dve.nop().then_inc(S("rank1_step"), 1)
            dve.wait_ge(S("degi_made"), 1)

            def over_root(i):
                dve.tensor_scalar(XN[:, i, :], XN[:, i, :], inv_out[:, i:i + 1], None, ALU.mult)\
                   .then_inc(S("hs_made"), 1)
            layer_norm_rows(3, X, over_root)
            dve.wait_ge(S("vec_in"), 48)

            def finish(j):
                b = j % 2
                dve.wait_ge(S("hg_made"), j + 1)
                dve.tensor_tensor(HG[b], bank(4 + b, P), BIAS[0:P, :], ALU.add).then_inc(S("hg_biased"), 1)
                dve.wait_ge(S("hg_biased"), j + 1)
                link(dve.bn_stats(stats[0:P, j, :], HG[b]))
                dve.bn_aggr(mv[0:P, j, :], stats[0:P, j, :]).then_inc(S("hg_stat"), 1)
                dve.wait_ge(S("hg_stat"), j + 1)
                dve.wait_ge(S("hg_rstd"), j + 1)
                link(dve.tensor_scalar(HG[b], HG[b], mv[0:P, j, 0:1], rstd[0:P, j:j + 1], ALU.subtract, ALU.mult))
                link(dve.tensor_tensor(HG[b], HG[b], GAMMA[0:P, :], ALU.mult))
                dve.tensor_tensor(HG[b], HG[b], BETA[0:P, :], ALU.add).then_inc(S("hg_shift"), 1)

            def add_layer(j):
                dve.wait_ge(S("hg_gelu"), j + 1)
                link(dve.tensor_tensor(X[:, j, :], X[:, j, :], HG[j % 2], ALU.add))
            for j in range(T):
                dve.wait_ge(S("agg_made"), j + 1)
                above_zero(dve, S("agg_turned"), j - 1)
                dve.tensor_scalar(AGG[j % 2], bank(j % 2, P), inv_in[:, j:j + 1], None, ALU.mult)\
                   .then_inc(S("agg_moved"), 1)
                if j:
                    if j > 2:
                        add_layer(j - 3)
                    finish(j - 1)
            add_layer(T - 3)
            finish(T - 1)
            add_layer(T - 2)
            add_layer(T - 1)

            layer_norm_stats(X)
            dve.wait_ge(S("agg_made"), T)
            dve.wait_ge(S("ln_rstd"), 4)
            for i in range(T):
                dve.tensor_scalar(XN[:, i, :], X[:, i, :], mv[0:P, i, 0:1], rstd[0:P, i:i + 1],
                                  ALU.subtract, ALU.mult).then_inc(S("xn_made"), 1)
            dve.wait_ge(S("xt_turned"), 3 * T)
            dve.wait_ge(S("xn_made"), 3 * T)
            layer_norm_stats(XN)
            dve.wait_ge(S("ln_rstd"), 5)
            dve.wait_ge(S("gam_in"), 16)
            for i in range(T):
                link(dve.tensor_scalar(XN[:, i, :], XN[:, i, :], mv[0:P, i, 0:1], rstd[0:P, i:i + 1],
                                       ALU.subtract, ALU.mult))
                dve.tensor_tensor(XN[:, i, :], XN[:, i, :], GAM1[0:P, :], ALU.mult).then_inc(S("xn_made"), 1)
            dve.wait_ge(S("log1_made"), 1)
            link(dve.memset(logits[:, :, :], -3.0e38))
            dve.tensor_copy(logits[:, :, 0:E1], bank(2, P, 8 * T).rearrange("p (i e) -> p i e", e=8)[:, :, 0:E1])\
               .then_inc(S("g1_step"), 1)
            dve.wait_ge(S("g1_step"), 1)
            for i in range(T):
                link(dve.max(top[:, i, :], logits[:, i, :]))
                link(dve.max_index(top_i[:, i, :], top[:, i, :], logits[:, i, :]))
            link(dve.tensor_copy(pick[:, :, :], top_i[:, :, 0:2]))
            dve.tensor_tensor(mask[:, 0, :, :], iota_b, pick[:, :, 0:1].to_broadcast([P, T, 8]),
                              ALU.is_equal).then_inc(S("log1_top"), 1)
            dve.tensor_tensor(logits[:, :, 0:E1], logits[:, :, 0:E1], top[:, :, 0:1].to_broadcast([P, T, E1]),
                              ALU.subtract).then_inc(S("g1_step"), 1)
            link(dve.tensor_tensor(gates[:, 1, :], top[:, :, 1], top[:, :, 0], ALU.subtract))
            dve.tensor_copy(logits[:, :, 6:7], gates[:, 1, :].unsqueeze(2)).then_inc(S("g1_step"), 1)
            dve.wait_ge(S("g1_exp"), 1)
            link(dve.tensor_reduce(gates[:, 0, :], logits[:, :, 0:E1], X_AXIS, ALU.add))
            link(dve.reciprocal(gates[:, 2, :], gates[:, 0, :]))
            dve.wait_ge(S("log1_top"), 1)
            link(dve.tensor_scalar(mask[:, 1, :, :], mask[:, 0, :, :], -1.0, 1.0, ALU.mult, ALU.add))
            link(dve.tensor_tensor(mask[:, 1, :, 0:E1], mask[:, 1, :, 0:E1], logits[:, :, 0:E1], ALU.mult))
            link(dve.tensor_reduce(gates[:, 1, :], mask[:, 1, :, 0:E1], X_AXIS, ALU.max))
            link(dve.tensor_tensor(gates[:, 1, :], gates[:, 1, :], gates[:, 2, :], ALU.mult))
            link(dve.tensor_tensor(gates[:, 1, :], gates[:, 1, :], gates[:, 2, :], ALU.add))
            link(dve.tensor_scalar(gates[:, 1, :], gates[:, 1, :], GATE_EPS, None, ALU.add))
            link(dve.reciprocal(gates[:, 3, :], gates[:, 1, :]))
            link(dve.tensor_tensor(gates[:, 0, :], gates[:, 2, :], gates[:, 3, :], ALU.mult))
            dve.wait_ge(S("rank1_made"), 1)
            slots_of([mask[:, 0, :, :]], MT1, E1, S("slot1_made"))

            def mix1(g):
                for k in range(LANES):
                    dve.wait_ge(S("yy_made"), g * LANES + k + 1)
                    above_zero(dve, yy_out[k], g * 16)
                    dve.tensor_copy(ys[k], bank(2 * k + 1)).then_inc(S("yy_moved"), 1)
            mix1(0)
            with dve.Fori(1, MT1 // LANES) as g:
                mix1(g)
            for i in range(T):
                add_rows(K0 * T + i, i, gates[:, 0, i:i + 1])
                dve.nop().then_inc(S("x_stored"), 1)


_INS = ["x", "src", "dst", "L0_gnn_W", "L0_ffn_gate_w", "L0_ffn_w1", "L0_ffn_w2", "L0_ffn_w3", "L0_ffn_n1",
        "L0_ffn_n2", "L1_gnn_W", "L1_gnn_b", "L1_gnn_gamma", "L1_gnn_beta", "L1_ffn_w_gating", "L1_ffn_gamma",
        "L1_ffn_w1", "L1_ffn_w2"]
_OUTS = [((N, D), "float32")]


def kernel(**inputs):
    import numpy as _np
    import concourse.bacc as _bacc
    from concourse import mybir as _mybir
    from concourse.bass_utils import run_bass_kernel_spmd as _run

    nc = _bacc.Bacc("TRN2", target_bir_lowering=False, num_devices=1)
    arrays, args = {}, []
    for name in _INS:
        a = _np.ascontiguousarray(inputs[name])
        arrays[f"in_{name}_dram"] = a
        args.append(nc.dram_tensor(f"in_{name}_dram", a.shape, _mybir.dt.from_np(a.dtype), kind="ExternalInput").ap())
    for i, (shape, dtype) in enumerate(_OUTS):
        dt = _mybir.dt.from_np(_np.dtype(dtype))
        args.append(nc.dram_tensor(f"out_{i}_dram", shape, dt, kind="ExternalOutput").ap())
    gnn_moe_kernel(nc, *args)
    r = _run(nc, [arrays], core_ids=[0])
    return r.results[0]["out_0_dram"]
```

```python
from contextlib import ExitStack

import concourse.bass as bass
from concourse import mybir

F32 = mybir.dt.float32
BF16 = mybir.dt.bfloat16
I32 = mybir.dt.int32
U32 = mybir.dt.uint32
U16 = mybir.dt.uint16
ALU = mybir.AluOpType
ACT = mybir.ActivationFunctionType
X_AXIS = mybir.AxisListType.X

N, E = 1250, 20000
P, T = 125, 10
D, C = 512, 4
HEADS, DH = 8, 64
EP, ET = 125, 160
HALF = N // 2
SHIFT = 12
WIN = 20
GEN_WIN = 32
GROUP = 4
NEG = -1.0e30
BIG = 10000.0
TM = 128
E0, H0, K0 = 8, 256, 2
MT0 = (K0 * N + E0 * (TM - 1)) // TM
E1, H1 = 6, 256
MT1 = (N + E1 * (TM - 1)) // TM
LANES = 3
LN_EPS, RMS_EPS, GATE_EPS = 1e-5, 1e-6, 1e-9
assert E == EP * ET and N == P * T and MT0 % LANES == 0 and MT1 % LANES == 0
assert WIN * EP < 2 ** SHIFT and GEN_WIN * EP < 2 ** SHIFT and ET % GEN_WIN == 0
PIECES = ((0, 512), (512, 1024), (1024, N))
TPIECES = ((0, 4), (4, 8), (8, 10))


def above_zero(eng, sem, value):
    if not (isinstance(value, int) and value <= 0):
        eng.wait_ge(sem, value)


def gnn_moe_kernel(nc, x, src, dst, L0_gnn_W, L0_ffn_gate_w, L0_ffn_w1, L0_ffn_w2, L0_ffn_w3,
                   L0_ffn_n1, L0_ffn_n2, L1_gnn_W, L1_gnn_b, L1_gnn_gamma, L1_gnn_beta,
                   L1_ffn_w_gating, L1_ffn_gamma, L1_ffn_w1, L1_ffn_w2, out):
    counts_d = nc.dram_tensor("counts_d", (N, N), F32).ap()
    logs_d = nc.dram_tensor("logs_d", (N, N), F32).ap()
    slots0_d = nc.dram_tensor("slots0_d", (MT0 * TM, D), F32).ap()
    slots1_d = nc.dram_tensor("slots1_d", (MT1 * TM, D), F32).ap()
    made0_d = nc.dram_tensor("made0_d", (MT0 * TM, D), F32).ap()
    made1_d = nc.dram_tensor("made1_d", (MT1 * TM, D), F32).ap()

    with ExitStack() as ctx:
        def sb(name, shape, dt=F32):
            return ctx.enter_context(nc.sbuf_tensor(name, shape, dt))

        def sem(name):
            return ctx.enter_context(nc.semaphore(name))

        X = sb("X", [P, T, D])
        XN = sb("XN", [P, T, D])
        XT = sb("XT", [128, C, N])
        R_W = sb("R_W", [128, 6144])
        R_B = sb("R_B", [128, 22500])
        R_A = sb("R_A", [128, 7680])
        Wqkv = R_W[:, :].rearrange("p (c n) -> p c n", c=C)
        QT = R_B[:, 0:5000].rearrange("p (j n) -> p j n", j=4)
        KT = R_B[:, 5000:10000].rearrange("p (j n) -> p j n", j=4)
        LNB = [R_B[0:P, 10000 + 1250 * b:10000 + 1250 * b + N] for b in range(2)]
        SC = [R_A[0:P, 1250 * b:1250 * b + N] for b in range(2)]
        PR = [R_A[0:P, 2500 + 1250 * b:2500 + 1250 * b + N] for b in range(2)]
        PT = [R_A[0:P, 5000 + 1250 * b:5000 + 1250 * b + N].rearrange("p (j n) -> p j n", j=T)
              for b in range(2)]
        oh_src = R_B[0:EP, 0:GROUP * HALF // 2].bitcast(BF16).rearrange("p (g n) -> p g n", g=GROUP)
        oh_dst = R_B[0:EP, 1250:1250 + GROUP * P // 2].bitcast(BF16).rearrange("p (g n) -> p g n", g=GROUP)
        iota_src = R_B[0:EP, 1500:1500 + 314].bitcast(U16)[:, 0:HALF]
        iota_dst = R_B[0:EP, 1820:1820 + 64].bitcast(U16)[:, 0:P]
        raw_idx = R_B[0:80, 2000:2500].bitcast(I32).rearrange("p (k e) -> p k e", k=2)
        idx_f = R_B[0:80, 2500:3250].rearrange("p (k e) -> p k e", k=3)
        src_f = R_B[0:80, 3250:3500]
        upper = R_B[0:80, 3500:3750]
        span_diag = R_B[0:80, 3750:4070].rearrange("p (k q) -> p k q", k=4)
        span_tmp = R_B[0:T, 4100:4100 + 5 * ET].rearrange("p (k t) -> p k t", k=5)
        packed = R_A[0:P, 0:HALF].bitcast(I32)
        unpacked = R_A[0:P, 650:650 + N].bitcast(I32)
        CT = R_A[0:P, 1900:1900 + N]
        lnCT = R_A[0:P, 3150:3150 + N]
        penalty = R_A[0:P, 4400:4400 + N]
        stage = R_A[0:P, 5650:5650 + N].rearrange("p (i n) -> p i n", i=T)
        idxT = R_B[0:EP, 6300:6300 + 3 * ET].rearrange("p (k t) -> p k t", k=3)
        win = R_B[0:EP, 6800:6800 + 3 * GEN_WIN].rearrange("p (k t) -> p k t", k=3)
        zero_rows = R_B[:, 7000:7512]
        ln_stage = R_B[0:P, 12500:12500 + N].rearrange("p (i n) -> p i n", i=T)
        sumCT = R_B[0:P, 5000:5000 + N]
        W1E = R_B[:, 0:8192].rearrange("p (e n) -> p e n", e=E0)
        W2E = R_B[:, 8192:12288].rearrange("p (e n) -> p e n", e=E0)
        W3E = R_B[:, 14308:22500].rearrange("p (e n) -> p e n", e=E0)
        N1B = R_W[:, 0:2048]
        N2B = R_W[:, 2048:4096]
        WG = R_W[:, 4096:6144].rearrange("p (c n) -> p c n", c=C)

        def lane(off, n):
            return [R_A[:, 2560 * k + off:2560 * k + off + n] for k in range(LANES)]

        xs, xsT, act1, h1n, h2n, hT, ys = (lane(0, 512), lane(512, 512), lane(1024, 256), lane(1280, 256),
                                           lane(1536, 256), lane(1792, 256), lane(2048, 512))
        CS_A = XT[0:P, :, :]
        CS_B = XN[:, :, :].rearrange("p i d -> p (i d)")[:, 0:C * N].rearrange("p (i n) -> p i n", i=C)
        CS_C = R_B[0:P, 10000:10000 + (T - 2 * C) * N].rearrange("p (i n) -> p i n", i=T - 2 * C)
        counts_of = [part[:, i, :] for part, n in ((CS_A, C), (CS_B, C), (CS_C, T - 2 * C)) for i in range(n)]
        HS = [R_B[0:P, 12544 + D * i:12544 + D * i + D] for i in range(T)]
        BIAS, GAMMA, BETA = (R_B[:, 6144 + 512 * k:6656 + 512 * k] for k in range(3))
        AGG = [R_A[0:P, 512 * k:512 * k + 512] for k in range(2)]
        AGT = [R_A[:, 1024 + 512 * k:1536 + 512 * k].rearrange("p (c n) -> p c n", c=C) for k in range(2)]
        HG = [R_A[0:P, 2048 + 512 * k:2560 + 512 * k] for k in range(2)]
        XM = [R_W[0:P, D * i:D * i + D] for i in range(8)] + [R_A[0:P, 3072 + D * k:3072 + D * k + D] for k in range(2)]
        W1B = R_B[:, 0:6144].rearrange("p (e n) -> p e n", e=E1)
        GAM1 = R_B[:, 7680:8192]
        W2B = R_B[:, 12544:18688].rearrange("p (e n) -> p e n", e=E1)
        rows = [R_A[0:P, D * n:D * n + D] if n < 12 else R_B[0:P, D * (n - 12):D * (n - 12) + D]
                for n in range(K0 * T)]

        count_rows = [R_W[0:P, 640 + N * k:640 + N * k + N] for k in range(4)]
        ident = sb("ident", [128, 128])
        Qst = R_W[:, 0:4 * P].rearrange("p (j n) -> p j n", j=4)
        tile_off = sb("tile_off", [128, T])
        bounds = sb("bounds", [80, 4])
        spans = sb("spans", [T, 8])
        ctl_f = sb("ctl_f", [1, 32])
        ctl = sb("ctl", [1, 32], I32)
        deg_in = sb("deg_in", [P, T])
        deg_out = sb("deg_out", [P, T])
        inv_in = sb("inv_in", [P, T])
        inv_out = sb("inv_out", [P, T])
        neg_max = sb("neg_max", [P, 4])
        den = sb("den", [P, 2])
        rden = sb("rden", [P, 2])
        head_out = R_W[0:P, 512:640].rearrange("p (b n) -> p b n", b=2)
        stats = sb("stats", [128, T, 6])
        mv = sb("mv", [128, T, 2])
        rstd = sb("rstd", [128, T])
        half_pow = sb("half_pow", [128, T])
        before = sb("before", [128, 128])
        ones = sb("ones", [128, 128])
        gate_w = sb("gate_w", [128, C, 8])
        logits = R_A[0:P, 6900:6980].rearrange("p (a b) -> p a b", a=10)
        top = R_A[0:P, 6980:7060].rearrange("p (a b) -> p a b", a=10)
        top_i = R_A[0:P, 7060:7140].bitcast(U32).rearrange("p (a b) -> p a b", a=10)
        pick = R_A[0:P, 7140:7160].rearrange("p (a b) -> p a b", a=10)
        iota8 = sb("iota8", [P, 8])
        iotaT = sb("iotaT", [1, MT0])
        mask = R_A[0:P, 7160:7400].rearrange("p (a b c) -> p a b c", a=3, b=10)
        place = R_A[0:128, 7400:7480].rearrange("p (a b) -> p a b", a=10)
        cnt = sb("cnt", [128, 5, 8])
        cnt_i = sb("cnt_i", [128, 8], I32)
        owner = R_B[0:1, 12288:12288 + 8 * MT0].rearrange("p (t e) -> p t e", e=8)
        owner_f = sb("owner_f", [1, MT0])
        owner_i = sb("owner_i", [1, MT0], I32)
        slot_f = sb("slot_f", [P, 2, T])
        slot = sb("slot", [P, 2, T], I32)
        gates = sb("gates", [P, 4, T])
        sq = [R_B[:, 12544 + H0 * k:12544 + H0 * k + H0] for k in range(LANES)]
        ssum = sb("ssum", [128, LANES])
        rms = sb("rms", [128, LANES])

        ps = ctx.enter_context(nc.psum_tensor("ps", [128, 8 * 512], F32))

        def bank(b, rows=128, cols=512, off=0):
            return ps[0:rows, 512 * b + off:512 * b + off + cols]

        normed = [XN[:, i, :] for i in range(T)]

        names = """x_in edges_in w_in wg_in consts zero_made zeros_out
            idx_step idx_turned span_step diag_made span_sums ctl_sums ctl_ready
            win_made hot slots_free gen_win gen_hot gen_free gen_step
            packed_out unpacked_out ct_made max_made pen_made ln_made lnct_made
            ct_turned lnct_turned ct_moved lnct_moved counts_out
            dve_chain ln_stat ln_rstd xn_made xt_turned xt_moved v_turned v_moved
            qk_made qk_moved q_staged s_made z_made p_made p_turned pt_moved_a pt_moved_v o_made o_moved
            rden_made x_added x_stored
            gate_in w1e_in w2e_in w3e_in nrm_in log_made mask_made rank_made gen_fold
            slot_made gate_step gate_exp rows_out xs_in0 xs_in1 xs_in2 xs_turned xs_moved h1_made g1_made
            ss_made rms_step rms_made n1_made h1_turned h1_moved h2_made g2_made ss2_made rms2_step
            rms2_made h2_scaled n2_made h2_turned h2_moved y_made y_moved y_out0 y_out1 y_out2
            counts_in logs_out vec_in hs_made agg_made agg_moved agg_turned agt_moved hg_made hg_biased
            hg_stat hg_rstd hg_shift hg_gelu
            gate1_in w1b_in w2b_in gam_in log1_made g1_step g1_exp rank1_made deg_out_made
            log1_top slot1_made rows1_out z_in0 z_in1 z_in2 z_turned z_moved hh_made gg_made gg_turned
            gg_moved yy_made yy_moved yy_out0 yy_out1 yy_out2
            out_done pool_chain rows_added degi_made"""
        s = {n: sem(n) for n in names.split()}
        rows_in = [sem(f"rows_in{k}") for k in range(T)]

        def S(n):
            return s[n]

        block = ctx.enter_context(nc.Block())

        count_rows_in = [sem(f"count_rows_in{k}") for k in range(4)]
        logs_in = [sem("logs_in0"), sem("logs_in1")]
        xs_in = [s["xs_in0"], s["xs_in1"], s["xs_in2"]]
        y_out = [s["y_out0"], s["y_out1"], s["y_out2"]]
        z_in = [s["z_in0"], s["z_in1"], s["z_in2"]]
        yy_out = [s["yy_out0"], s["yy_out1"], s["yy_out2"]]
        @block.sync
        def _(sp):
            sp.dma_start(raw_idx[:, 0, :], dst.rearrange("(q e) -> q e", q=80)).then_inc(S("edges_in"), 16)
            sp.dma_start(raw_idx[:, 1, :], src.rearrange("(q e) -> q e", q=80)).then_inc(S("edges_in"), 16)
            sp.dma_start(X[:, :, :], x.rearrange("(i p) d -> p i d", p=P)).then_inc(S("x_in"), 16)
            sp.dma_start(Wqkv, L0_gnn_W.rearrange("(c p) n -> p c n", c=C)).then_inc(S("w_in"), 16)
            sp.dma_start(gate_w[:, :, :], L0_ffn_gate_w.rearrange("(c p) n -> p c n", c=C)).then_inc(S("gate_in"), 16)
            sp.wait_ge(S("zero_made"), 1)
            for d, n in ((slots0_d, MT0), (slots1_d, MT1)):
                sp.dma_start(d.rearrange("(t p) d -> p t d", p=TM),
                             zero_rows.unsqueeze(1).to_broadcast([TM, n, D])).then_inc(S("zeros_out"), 16)

            def store_counts(b):
                sp.wait_ge(S("ct_moved"), 3 * b + 3)
                sp.dma_start(counts_d[:, bass.ds(b * P, P)].rearrange("(i p) d -> p i d", p=P),
                             stage).then_inc(S("counts_out"), 16)
                sp.wait_ge(S("lnct_moved"), 3 * b + 3)
                sp.dma_start(logs_d[:, bass.ds(b * P, P)].rearrange("(i p) d -> p i d", p=P),
                             ln_stage).then_inc(S("logs_out"), 16)
            with sp.Fori(0, T) as b:
                store_counts(b)

            def load_logs(i, b, guard):
                if guard:
                    sp.wait_ge(S("z_made"), i * HEADS - HEADS)
                sp.dma_start(LNB[b], logs_d[bass.ds(i * P, P), :]).then_inc(logs_in[b], 16)
            sp.wait_ge(S("logs_out"), 16 * T)
            load_logs(0, 0, False)
            load_logs(1, 1, False)
            sp.wait_ge(S("qk_made"), 24)
            sp.wait_ge(S("v_turned"), T)
            for i in range(T):
                above_zero(sp, S("deg_out_made"), i - 3)
                sp.dma_start(count_rows[i % 4], counts_d[i * P:i * P + P, :]).then_inc(count_rows_in[i % 4], 16)
            for e in range(E0):
                sp.dma_start(W3E[:, e, :].rearrange("p (c n) -> p c n", c=2),
                             L0_ffn_w3[e].rearrange("(c p) n -> p c n", c=2)).then_inc(S("w3e_in"), 16)
            with sp.Fori(1, T // 2) as ii:
                load_logs(2 * ii, 0, True)
                load_logs(2 * ii + 1, 1, True)
            sp.wait_ge(S("x_added"), T * HEADS)
            for e in range(E0):
                sp.dma_start(W1E[:, e, :].rearrange("p (c n) -> p c n", c=C),
                             L0_ffn_w1[e].rearrange("(c p) n -> p c n", c=C)).then_inc(S("w1e_in"), 16)
            for n_, dest in ((L0_ffn_n1, N1B), (L0_ffn_n2, N2B)):
                sp.dma_start(dest, n_.rearrange("e h -> (e h)").partition_broadcast(128)).then_inc(S("nrm_in"), 16)
            for e in range(E0):
                sp.dma_start(W2E[:, e, :].rearrange("p (c n) -> p c n", c=2),
                             L0_ffn_w2[e].rearrange("(c p) n -> p c n", c=2)).then_inc(S("w2e_in"), 16)
            sp.dma_start(WG, L1_gnn_W.rearrange("(c p) n -> p c n", c=C)).then_inc(S("wg_in"), 16)

            def mix_loads(slots, made, groups, ins, turned, outs, moved, meanwhile=None):
                def load(t, k, wait):
                    if wait is not None:
                        sp.wait_ge(turned, wait)
                    sp.dma_start(xs[k][:, :], slots[bass.ds(t * TM, TM), :]).then_inc(ins[k], 16)

                def store(t, k, g):
                    sp.wait_ge(moved, g * LANES + k + 1)
                    sp.dma_start(made[bass.ds(t * TM, TM), :], ys[k][:, :]).then_inc(outs[k], 16)
                for k in range(LANES):
                    load(k, k, None)
                with sp.Fori(0, groups - 1) as g:
                    for k in range(LANES):
                        load(g * LANES + LANES + k, k, g * LANES + k + 1)
                    for k in range(LANES):
                        store(g * LANES + k, k, g)
                if meanwhile is not None:
                    meanwhile()
                for k in range(LANES):
                    store((groups - 1) * LANES + k, k, groups - 1)
            sp.wait_ge(S("log_made"), 1)
            sp.wait_ge(S("counts_out"), 16 * T)
            sp.dma_start(CS_A, counts_d[0:C * P, :].rearrange("(i p) d -> p i d", p=P)).then_inc(S("counts_in"), 16)
            sp.wait_ge(S("rows_out"), 16 * K0 * T)

            def load_counts():
                sp.dma_start(CS_B, counts_d[C * P:2 * C * P, :].rearrange("(i p) d -> p i d", p=P))\
                  .then_inc(S("counts_in"), 16)
            mix_loads(slots0_d, made0_d, MT0 // LANES, xs_in, S("xs_turned"), y_out, S("y_moved"), load_counts)
            sp.wait_ge(S("y_made"), MT0)
            sp.wait_ge(rows_in[T // 2], 16 * K0)
            sp.dma_start(CS_C, counts_d[2 * C * P:N, :].rearrange("(i p) d -> p i d", p=P)).then_inc(S("counts_in"), 16)
            for v, dest in ((L1_gnn_b, BIAS), (L1_gnn_gamma, GAMMA), (L1_gnn_beta, BETA)):
                sp.dma_start(dest, v.partition_broadcast(128)).then_inc(S("vec_in"), 16)
            sp.wait_ge(S("agg_made"), 1)
            for e in range(E1):
                sp.dma_start(W1B[:, e, :].rearrange("p (c n) -> p c n", c=C),
                             L1_ffn_w1[e].rearrange("(c p) n -> p c n", c=C)).then_inc(S("w1b_in"), 16)
            sp.dma_start(GAM1, L1_ffn_gamma.partition_broadcast(128)).then_inc(S("gam_in"), 16)
            sp.wait_ge(S("log_made"), 1)
            sp.dma_start(gate_w[:, :, 0:E1], L1_ffn_w_gating.rearrange("(c p) n -> p c n", c=C))\
              .then_inc(S("gate1_in"), 16)
            sp.wait_ge(S("agg_made"), T)
            for e in range(E1):
                sp.dma_start(W2B[:, e, :].rearrange("p (c n) -> p c n", c=2),
                             L1_ffn_w2[e].rearrange("(c p) n -> p c n", c=2)).then_inc(S("w2b_in"), 16)
            sp.wait_ge(S("rows1_out"), 16 * T)
            mix_loads(slots1_d, made1_d, MT1 // LANES, z_in, S("z_turned"), yy_out, S("yy_moved"))
            for i in range(T):
                sp.wait_ge(S("x_stored"), i + 1)
                sp.dma_start(out[P * i:P * i + P, :], X[:, i, :]).then_inc(S("out_done"), 16)
            sp.wait_ge(S("out_done"), 16 * T)
            sp.wait_ge(S("zeros_out"), 32)

        @block.tensor
        def _(pe):
            pe.wait_ge(S("consts"), 1)
            pe.wait_ge(S("idx_step"), 5)
            for k in range(3):
                for r in range(2):
                    ins = pe.transpose(bank(6, EP, 80, (2 * k + r) * 80), idx_f[:, k, EP * r:EP * r + EP],
                                       ident[0:80, 0:80])
            ins.then_inc(S("idx_turned"), 1)
            pe.wait_ge(S("diag_made"), 4)
            pe.matmul(bank(7, T, 320), ones[0:80, 0:T], span_diag.rearrange("p k q -> p (k q)"),
                      start=True, stop=True).then_inc(S("span_sums"), 1)
            pe.wait_ge(S("span_step"), 8)
            for k in range(2):
                ins = pe.matmul(bank(7, 1, T, 320 + 16 * k), spans[:, 6 + k:7 + k], ident[0:T, 0:T],
                                start=True, stop=True)
            ins.then_inc(S("ctl_sums"), 1)
            pe.wait_ge(S("ctl_ready"), 1)
            all_hold = pe.value_load(ctl[0:1, T:T + 1], min_val=0, max_val=1)

            def count_group(g0, buf, hot, free, first=False, last=False):
                for k in range(GROUP):
                    pe.wait_ge(hot, g0 + k + 1)
                    a, z = first and k == 0, last and k == GROUP - 1
                    pe.matmul(bank(2 * buf, P, 512), oh_dst[:, k, :], oh_src[:, k, 0:512], start=a, stop=z,
                              skip_group_check=True)
                    pe.matmul(bank(2 * buf + 1, P, HALF - 512), oh_dst[:, k, :], oh_src[:, k, 512:HALF],
                              start=a, stop=z, skip_group_check=True).then_inc(free, 1)

            def count_window(g0, tiles, buf, *sems):
                count_group(g0, buf, *sems, first=True)
                with pe.Fori(1, tiles // GROUP - 1) as k:
                    count_group(g0 + k * GROUP, buf, *sems)
                count_group(g0 + (tiles - GROUP), buf, *sems, last=True)

            def turn_counts(b):
                for sourced, source, turned, moved in ((S("ct_made"), CT, S("ct_turned"), S("ct_moved")),
                                                       (S("lnct_made"), lnCT, S("lnct_turned"), S("lnct_moved"))):
                    pe.wait_ge(sourced, b + 1)
                    if source is CT:
                        above_zero(pe, S("lnct_moved"), 3 * b)
                    else:
                        pe.wait_ge(S("ct_moved"), 3 * b + 3)
                    for q, (a, z) in enumerate(TPIECES):
                        for i in range(a, z):
                            ins = pe.transpose(bank(4 + q, P, P, (i - a) * P), source[:, i * P:i * P + P],
                                               ident[0:P, 0:P])
                        ins.then_inc(turned, 1)

            def fast_block(b, buf, after):
                above_zero(pe, S("packed_out"), b - 1)
                count_window(b * WIN, WIN, buf, S("hot"), S("slots_free"))
                if after is not None:
                    turn_counts(after)

            with pe.If(all_hold):
                pe.nop().then_inc(S("slots_free"), GROUP)
                fast_block(0, 0, None)
                fast_block(1, 1, 0)
                with pe.Fori(2, T, 2) as b:
                    fast_block(b, 0, b - 1)
                    fast_block(b + 1, 1, b)
                turn_counts(T - 1)
            with pe.Else():
                pe.nop().then_inc(S("gen_free"), GROUP)

                def general_block(b):
                    for w in range(ET // GEN_WIN):
                        above_zero(pe, S("gen_step"), b * (ET // GEN_WIN) + w)
                        count_window(b * ET + w * GEN_WIN, GEN_WIN, 0, S("gen_hot"), S("gen_free"))
                    turn_counts(b)
                general_block(0)
                with pe.Fori(1, T) as b:
                    general_block(b)
            pe.end_ifs()

            def route(i, n_exp):
                for c in range(C):
                    ins = pe.matmul(bank(2, P, n_exp, 8 * i), XT[:, c, i * P:i * P + P],
                                    gate_w[:, c, 0:n_exp], start=c == 0, stop=c == C - 1,
                                    skip_group_check=True)
                return ins

            def turn_rows(made0, n0, source, n_exp=0):
                for i in range(T):
                    pe.wait_ge(S("xn_made"), made0 + i + 1)
                    above_zero(pe, S("xt_moved"), n0 + i - 1 if i > 1 else n0)
                    for c in range(C):
                        ins = pe.transpose(bank(i % 2, 128, P, c * P), source[i][:, c * 128:c * 128 + 128],
                                           ident[0:P, 0:P])
                    ins.then_inc(S("xt_turned"), 1)
                    if n_exp and i:
                        pe.wait_ge(S("xt_moved"), n0 + i)
                        route(i - 1, n_exp)

            pe.wait_ge(S("w_in"), 16)
            pe.wait_ge(S("packed_out"), T)
            turn_rows(0, 0, normed)
            pe.wait_ge(S("xt_moved"), T)
            pe.wait_ge(S("lnct_moved"), 3 * T)
            n = 0
            for part in (1, 0):
                for j in range(4):
                    for q, (a, z) in enumerate(PIECES):
                        above_zero(pe, S("qk_moved"), n - 3)
                        for c in range(C):
                            w = part * D + j * 128
                            ins = pe.matmul(bank(2 + n % 4, 128, z - a), Wqkv[:, c, w:w + 128], XT[:, c, a:z],
                                            start=c == 0, stop=c == C - 1)
                        ins.then_inc(S("qk_made"), 1)
                        n += 1
            for i in range(T):
                above_zero(pe, S("v_moved"), i - 1)
                for c in range(C):
                    ins = pe.matmul(bank(i % 2, P), XT[:, c, i * P:i * P + P], Wqkv[:, c, 2 * D:3 * D],
                                    start=c == 0, stop=c == C - 1)
                ins.then_inc(S("v_turned"), 1)
            pe.wait_ge(S("v_moved"), T)
            pe.wait_ge(S("qk_moved"), 24)

            def scores(u, h, buf, j_staged, pieces=(0, 1, 2)):
                r = DH * (h % 2)
                if pieces[0] == 0:
                    pe.wait_ge(S("q_staged"), j_staged)
                    above_zero(pe, S("z_made"), u - 1)
                for q in pieces:
                    a, z = PIECES[q]
                    ins = pe.matmul(bank(3 * buf + q, P, z - a), Qst[r:r + DH, h // 2, :],
                                    KT[r:r + DH, h // 2, a:z], start=True, stop=True)
                if pieces[-1] == 2:
                    ins.then_inc(S("s_made"), 1)

            def head(u, i, h, more, guard=True):
                buf = h % 2
                pe.wait_ge(S("p_made"), u + 1)
                for q, (a, z) in enumerate(TPIECES):
                    if q == 0 and guard:
                        pe.wait_ge(S("pt_moved_a"), 2 * u)
                    if q == 1 and guard:
                        pe.wait_ge(S("o_moved"), u)
                    if q == 2:
                        pe.wait_ge(S("pt_moved_a"), 2 * u + 1)
                    for jj in range(a, z):
                        ins = pe.transpose(bank(6 + q % 2, P, P, (jj - a) * P), PR[buf][:, jj * P:jj * P + P],
                                           ident[0:P, 0:P])
                    ins.then_inc(S("p_turned"), 1)
                    if more and q != 1:
                        scores(u + 2, (h + 2) % HEADS, buf, i * 4 + (h + 2) // 2 + 1, (0,) if q == 0 else (1, 2))
                pe.wait_ge(S("pt_moved_a"), 2 * u + 2)
                pe.wait_ge(S("pt_moved_v"), u + 1)
                for jj in range(T):
                    ins = pe.matmul(bank(7, P, DH), PT[buf][:, jj, :],
                                    XN[:, jj, h * DH:h * DH + DH], start=jj == 0, stop=jj == T - 1)
                ins.then_inc(S("o_made"), 1)

            scores(0, 0, 0, 1)
            scores(1, 1, 1, 1)
            for h in range(HEADS):
                head(h, 0, h, True, guard=h > 0)
            with pe.Fori(1, T - 1) as i:
                for h in range(HEADS):
                    head(i * HEADS + h, i, h, True)
            for h in range(HEADS):
                head((T - 1) * HEADS + h, T - 1, h, h < 6)
            pe.wait_ge(S("x_added"), T * HEADS)

            def rank(mask_sem, mask_v, m, made):
                pe.wait_ge(mask_sem, mask_v)
                pe.matmul(bank(3, P, 8 * T), before[0:P, 0:P], m, start=True, stop=True)
                pe.matmul(bank(3, 128, 8 * T, 128), ones[0:P, :], m, start=True, stop=True,
                          skip_group_check=True).then_inc(made, 1)

            pe.wait_ge(S("gate_in"), 16)
            turn_rows(T, T, normed, E0)
            pe.wait_ge(S("xt_moved"), 2 * T)
            route(T - 1, E0).then_inc(S("log_made"), 1)
            rank(S("mask_made"), 3, mask[:, 2, :, :].rearrange("p i e -> p (i e)"), S("rank_made"))
            pe.wait_ge(S("slot_made"), 1)
            pe.wait_ge(S("w1e_in"), 16 * E0)

            def turn_lane(k, bk, source, n, turned, rows_=TM):
                for c in range(n):
                    ins = pe.transpose(bank(bk, 128, rows_, c * rows_), source[:, c * 128:c * 128 + 128],
                                       ident[0:rows_, 0:rows_])
                ins.then_inc(turned, 1)

            def expert_product(k, bk, lhs, weights, e, n, width, made):
                for c in range(n):
                    ins = pe.matmul(bank(bk, TM, width), lhs[:, c * TM:c * TM + TM],
                                    weights.rearrange("p e n -> p (e n)")[:, bass.ds(e * (n * width) + c * width, width)],
                                    start=c == 0, stop=c == n - 1)
                ins.then_inc(made, 1)

            def mix0(g, guard):
                lanes_ = range(LANES)
                e = [pe.value_load(owner_i[0:1, bass.ds(g * LANES + k, 1)], min_val=0, max_val=E0 - 1)
                     for k in lanes_]
                for k in lanes_:
                    pe.wait_ge(xs_in[k], 16 * g + 16)
                    turn_lane(k, 2 * k, xs[k], C, S("xs_turned"))
                for k in lanes_:
                    pe.wait_ge(S("xs_moved"), g * LANES + k + 1)
                    if guard:
                        pe.wait_ge(S("y_moved"), g * LANES + k + 1 - LANES)
                    expert_product(k, 2 * k + 1, xsT[k], W1E, e[k], C, H0, S("h1_made"))
                for k in lanes_:
                    pe.wait_ge(S("n1_made"), g * LANES + k + 1)
                    turn_lane(k, 2 * k, h1n[k], 2, S("h1_turned"))
                for k in lanes_:
                    pe.wait_ge(S("h1_moved"), g * LANES + k + 1)
                    if not guard and k == 0:
                        pe.wait_ge(S("w2e_in"), 16 * E0)
                        pe.wait_ge(S("w3e_in"), 16 * E0)
                    expert_product(k, 2 * k + 1, hT[k], W2E, e[k], 2, H0, S("h2_made"))
                for k in lanes_:
                    pe.wait_ge(S("n2_made"), g * LANES + k + 1)
                    turn_lane(k, 2 * k, h2n[k], 2, S("h2_turned"))
                for k in lanes_:
                    pe.wait_ge(S("h2_moved"), g * LANES + k + 1)
                    expert_product(k, 2 * k + 1, hT[k], W3E, e[k], 2, D, S("y_made"))
            mix0(0, False)
            with pe.Fori(1, MT0 // LANES) as g:
                mix0(g, True)
            pe.wait_ge(S("y_moved"), MT0)

            pe.wait_ge(S("counts_in"), 48)
            pe.wait_ge(S("hs_made"), T)
            pe.wait_ge(S("wg_in"), 16)

            def project(j):
                b = j % 2
                pe.wait_ge(S("agg_moved"), j + 1)
                above_zero(pe, S("agt_moved"), j - 1)
                for c in range(C):
                    ins = pe.transpose(bank(2 + b, 128, P, c * P), AGG[b][:, c * 128:c * 128 + 128],
                                       ident[0:P, 0:P])
                ins.then_inc(S("agg_turned"), 1)
                pe.wait_ge(S("agt_moved"), j + 1)
                above_zero(pe, S("hg_biased"), j - 1)
                for c in range(C):
                    ins = pe.matmul(bank(4 + b, P), AGT[b][:, c, 0:P], WG[:, c, :], start=c == 0, stop=c == C - 1)
                ins.then_inc(S("hg_made"), 1)
            for j in range(T):
                above_zero(pe, S("agg_moved"), j - 1)
                for i in range(T):
                    ins = pe.matmul(bank(j % 2, P), counts_of[i][:, j * P:j * P + P], HS[i],
                                    start=i == 0, stop=i == T - 1)
                ins.then_inc(S("agg_made"), 1)
                if j:
                    project(j - 1)
            project(T - 1)

            pe.wait_ge(S("gate1_in"), 16)
            turn_rows(2 * T, 2 * T, XM, E1)
            pe.wait_ge(S("xt_moved"), 3 * T)
            route(T - 1, E1).then_inc(S("log1_made"), 1)
            rank(S("log1_top"), 1, mask[:, 0, :, :].rearrange("p i e -> p (i e)"), S("rank1_made"))
            pe.wait_ge(S("slot1_made"), 1)
            pe.wait_ge(S("w1b_in"), 16 * E1)
            pe.wait_ge(S("w2b_in"), 16 * E1)

            def mix1(g, guard):
                lanes_ = range(LANES)
                e = [pe.value_load(owner_i[0:1, bass.ds(g * LANES + k, 1)], min_val=0, max_val=E1 - 1)
                     for k in lanes_]
                for k in lanes_:
                    pe.wait_ge(z_in[k], 16 * g + 16)
                    turn_lane(k, 2 * k, xs[k], C, S("z_turned"))
                for k in lanes_:
                    pe.wait_ge(S("z_moved"), g * LANES + k + 1)
                    if guard:
                        pe.wait_ge(S("yy_moved"), g * LANES + k + 1 - LANES)
                    expert_product(k, 2 * k + 1, xsT[k], W1B, e[k], C, H1, S("hh_made"))
                for k in lanes_:
                    pe.wait_ge(S("gg_made"), g * LANES + k + 1)
                    turn_lane(k, 2 * k, act1[k], 2, S("gg_turned"))
                for k in lanes_:
                    pe.wait_ge(S("gg_moved"), g * LANES + k + 1)
                    expert_product(k, 2 * k + 1, hT[k], W2B, e[k], 2, D, S("yy_made"))
            mix1(0, False)
            with pe.Fori(1, MT1 // LANES) as g:
                mix1(g, True)

        @block.scalar
        def _(act):
            act.wait_ge(S("ctl_ready"), 1)
            all_hold = act.value_load(ctl[0:1, T:T + 1], min_val=0, max_val=1)

            def move_packed(b, buf):
                act.wait_ge(S("slots_free"), b * WIN + (WIN + GROUP))
                above_zero(act, S("unpacked_out"), b)
                act.activation(packed, ps[0:P, 1024 * buf:1024 * buf + HALF], ACT.Copy)\
                   .then_inc(S("packed_out"), 1)

            def counts_and_logs(b):
                act.wait_ge(S("unpacked_out"), b + 1)
                above_zero(act, S("lnct_turned"), 3 * b)
                act.activation(CT, unpacked, ACT.Copy, accum_out=deg_in[:, bass.ds(b, 1)])\
                   .then_inc(S("ct_made"), 1)
                act.wait_ge(S("max_made"), b + 1)
                act.activation(lnCT, lnCT, ACT.Ln).then_inc(S("ln_made"), 1)
                above_zero(act, S("counts_out"), b * 16)
                for q, (a, z) in enumerate(TPIECES):
                    act.wait_ge(S("ct_turned"), 3 * b + q + 1)
                    act.activation(stage[:, a:z, :],
                                   bank(4 + q, P, (z - a) * P).rearrange("p (i n) -> p i n", n=P), ACT.Copy)\
                       .then_inc(S("ct_moved"), 1)
                above_zero(act, S("logs_out"), b * 16)
                for q, (a, z) in enumerate(TPIECES):
                    act.wait_ge(S("lnct_turned"), 3 * b + q + 1)
                    act.activation(ln_stage[:, a:z, :],
                                   bank(4 + q, P, (z - a) * P).rearrange("p (i n) -> p i n", n=P), ACT.Copy)\
                       .then_inc(S("lnct_moved"), 1)

            with act.If(all_hold):
                move_packed(0, 0)
                counts_and_logs(0)
                move_packed(1, 1)
                with act.Fori(2, T, 2) as b:
                    counts_and_logs(b - 1)
                    move_packed(b, 0)
                    counts_and_logs(b)
                    move_packed(b + 1, 1)
                counts_and_logs(T - 1)
            with act.Else():
                counts_and_logs(0)
                with act.Fori(1, T) as b:
                    counts_and_logs(b)
                act.wait_ge(S("gen_free"), T * ET + GROUP)
                act.nop().then_inc(S("packed_out"), T)
            act.end_ifs()

            def move_rows(n0):
                for i in range(T):
                    act.wait_ge(S("xt_turned"), n0 + i + 1)
                    act.activation(XT[:, :, i * P:i * P + P],
                                   bank(i % 2, 128, C * P).rearrange("p (c n) -> p c n", c=C), ACT.Copy)\
                       .then_inc(S("xt_moved"), 1)
            move_rows(0)
            act.wait_ge(S("zeros_out"), 32)
            n = 0
            for part in (1, 0):
                for j in range(4):
                    for q, (a, z) in enumerate(PIECES):
                        act.wait_ge(S("qk_made"), n + 1)
                        act.activation((KT if part else QT)[:, j, a:z], bank(2 + n % 4, 128, z - a), ACT.Copy,
                                       scale=1.0 if part else DH ** -0.5).then_inc(S("qk_moved"), 1)
                        n += 1

            def exponential(u, h, guard):
                buf = h % 2
                act.wait_ge(S("z_made"), u + 1)
                if guard:
                    act.wait_ge(S("p_turned"), 3 * u - 3)
                act.activation(PR[buf], SC[buf], ACT.Exp, bias=neg_max[:, h % 4:h % 4 + 1], scale=-1.0,
                               accum_out=den[:, buf:buf + 1]).then_inc(S("p_made"), 1)

            def move_turned(u, h):
                buf = h % 2
                for q in (0, 2):
                    a, z = TPIECES[q]
                    act.wait_ge(S("p_turned"), 3 * u + q + 1)
                    if q == 0:
                        above_zero(act, S("o_made"), u - 1)
                    act.activation(PT[buf][:, a:z, :],
                                   bank(6 + q % 2, P, (z - a) * P).rearrange("p (i n) -> p i n", n=P), ACT.Copy)\
                       .then_inc(S("pt_moved_a"), 1)

            def move_output(u, h):
                act.wait_ge(S("o_made"), u + 1)
                act.wait_ge(S("rden_made"), 2 * u + 2)
                above_zero(act, S("x_added"), u - 1)
                act.activation(head_out[:, h % 2, :], bank(7, P, DH), ACT.Copy, scale=rden[:, h % 2:h % 2 + 1])\
                   .then_inc(S("o_moved"), 1)
            exponential(0, 0, False)
            for h in range(HEADS):
                move_turned(h, h)
                exponential(h + 1, h + 1, h >= 1)
                move_output(h, h)
            with act.Fori(1, T - 1) as i:
                for h in range(HEADS):
                    move_turned(i * HEADS + h, h)
                    exponential(i * HEADS + h + 1, h + 1, True)
                    move_output(i * HEADS + h, h)
            for h in range(HEADS):
                move_turned((T - 1) * HEADS + h, h)
                if h < HEADS - 1:
                    exponential((T - 1) * HEADS + h + 1, h + 1, True)
                move_output((T - 1) * HEADS + h, h)

            move_rows(T)
            act.wait_ge(S("gate_step"), 1)
            act.activation(gates[:, 0, :], gates[:, 0, :], ACT.Exp).then_inc(S("gate_exp"), 1)

            def mix0(g):
                lanes_ = range(LANES)
                for k in lanes_:
                    act.wait_ge(S("xs_turned"), g * LANES + k + 1)
                    act.activation(xsT[k], bank(2 * k), ACT.Copy).then_inc(S("xs_moved"), 1)
                for k in lanes_:
                    act.wait_ge(S("h1_made"), g * LANES + k + 1)
                    act.activation(act1[k], bank(2 * k + 1, TM, H0), ACT.Gelu).then_inc(S("g1_made"), 1)
                for k in lanes_:
                    act.wait_ge(S("h1_turned"), g * LANES + k + 1)
                    act.activation(hT[k], bank(2 * k, 128, 256), ACT.Copy).then_inc(S("h1_moved"), 1)
                for k in lanes_:
                    act.wait_ge(S("h2_made"), g * LANES + k + 1)
                    act.activation(act1[k], bank(2 * k + 1, TM, H0), ACT.Gelu).then_inc(S("g2_made"), 1)
                for k in lanes_:
                    act.wait_ge(S("h2_turned"), g * LANES + k + 1)
                    act.activation(hT[k], bank(2 * k, 128, 256), ACT.Copy).then_inc(S("h2_moved"), 1)
            with act.Fori(0, MT0 // LANES) as g:
                mix0(g)

            for j in range(T):
                b = j % 2
                act.wait_ge(S("agg_turned"), j + 1)
                act.activation(AGT[b][:, :, 0:P],
                               bank(2 + b, 128, C * P).rearrange("p (c n) -> p c n", c=C), ACT.Copy)\
                   .then_inc(S("agt_moved"), 1)
                if j:
                    act.wait_ge(S("hg_shift"), j)
                    act.activation(HG[1 - b], HG[1 - b], ACT.Gelu).then_inc(S("hg_gelu"), 1)
            act.wait_ge(S("hg_shift"), T)
            act.activation(HG[1], HG[1], ACT.Gelu).then_inc(S("hg_gelu"), 1)

            move_rows(2 * T)
            act.wait_ge(S("g1_step"), 3)
            act.activation(logits[:, :, 0:E1], logits[:, :, 0:E1], ACT.Exp).then_inc(S("g1_exp"), 1)

            def mix1(g):
                lanes_ = range(LANES)
                for k in lanes_:
                    act.wait_ge(S("z_turned"), g * LANES + k + 1)
                    act.activation(xsT[k], bank(2 * k), ACT.Copy).then_inc(S("z_moved"), 1)
                for k in lanes_:
                    act.wait_ge(S("hh_made"), g * LANES + k + 1)
                    act.activation(act1[k], bank(2 * k + 1, TM, H1), ACT.Gelu).then_inc(S("gg_made"), 1)
                for k in lanes_:
                    act.wait_ge(S("gg_turned"), g * LANES + k + 1)
                    act.activation(hT[k], bank(2 * k, 128, 256), ACT.Copy).then_inc(S("gg_moved"), 1)
            with act.Fori(0, MT1 // LANES) as g:
                mix1(g)

        @block.gpsimd
        def _(pool):
            c = [0]

            def link(ins):
                c[0] += 1
                ins.then_inc(S("pool_chain"), 1)
                pool.wait_ge(S("pool_chain"), c[0])
            pool.memset(zero_rows, 0.0).then_inc(S("zero_made"), 1)
            pool.memset(ident[:, :], 0.0)
            pool.memset(ones[:, :], 1.0)
            pool.memset(half_pow[:, :], -0.5)
            link(pool.iota(tile_off[:, :], [[P, T]], base=0, channel_multiplier=0,
                           allow_small_or_imprecise_dtypes=True))
            pool.iota(iota_src, [[1, HALF]], base=0, channel_multiplier=0)
            pool.iota(iota_dst, [[1, P]], base=0, channel_multiplier=0)
            pool.iota(iota8[:, :], [[1, 8]], base=0, channel_multiplier=0, allow_small_or_imprecise_dtypes=True)
            pool.iota(iotaT[:, :], [[1, MT0]], base=0, channel_multiplier=0, allow_small_or_imprecise_dtypes=True)
            pool.iota(span_tmp[:, 0, :], [[1, 2], [2, 80]], base=0, channel_multiplier=0,
                      allow_small_or_imprecise_dtypes=True)
            pool.iota(span_tmp[:, 1, :], [[1, 2], [2, 80]], base=int(BIG), channel_multiplier=0,
                      allow_small_or_imprecise_dtypes=True)
            link(pool.iota(spans[:, 0:2], [[P, 2]], base=0, channel_multiplier=P,
                           allow_small_or_imprecise_dtypes=True))
            pool.affine_select(out=before[:, :], in_=ones[:, :], compare_op=ALU.is_gt, fill=0.0, base=0,
                               pattern=[[1, 128]], channel_multiplier=-1)
            pool.affine_select(out=ident[:, :], in_=ident[:, :], compare_op=ALU.not_equal, fill=1.0, base=0,
                               pattern=[[-1, 128]], channel_multiplier=1).then_inc(S("consts"), 1)

            def rstd_all(waited, n, eps, made):
                pool.wait_ge(waited, n)
                link(pool.tensor_scalar(rstd[0:P, :], mv[0:P, :, 1], 1.0, eps, ALU.mult, ALU.add))
                pool.tensor_tensor(rstd[0:P, :], rstd[0:P, :], half_pow[0:P, :], ALU.pow).then_inc(made, 1)
            rstd_all(S("ln_stat"), T, LN_EPS, S("ln_rstd"))


            pool.wait_ge(S("qk_moved"), 24)
            for j in range(4):
                pool.tensor_copy(Qst[:, j, :], QT[:, j, 0:P]).then_inc(S("q_staged"), 1)

            def add_heads(i, stage_next):
                for h in range(HEADS):
                    if stage_next and h % 2 == 0:
                        j = h // 2
                        pool.wait_ge(S("s_made"), i * HEADS + h + 2)
                        pool.tensor_copy(Qst[:, j, :], QT[:, j, bass.ds(i * P + P, P)]).then_inc(S("q_staged"), 1)
                    xa = X[:, :, :].rearrange("p i d -> p (i d)")[:, bass.ds(i * D + h * DH, DH)]
                    pool.wait_ge(S("o_moved"), i * HEADS + h + 1)
                    pool.tensor_tensor(xa, xa, head_out[:, h % 2, :], ALU.add).then_inc(S("x_added"), 1)
            with pool.Fori(0, T - 1) as i:
                add_heads(i, True)
            add_heads(T - 1, False)

            rstd_all(S("ln_stat"), 2 * T, LN_EPS, S("ln_rstd"))
            pool.wait_ge(S("slot_made"), 1)
            pool.wait_ge(S("zeros_out"), 32)
            pool.wait_ge(S("xn_made"), 2 * T)
            for k in range(K0):
                for i in range(T):
                    pool.indirect_dma_start(slots0_d, bass.IndirectOffsetOnAxis(ap=slot[:, k, i:i + 1], axis=0),
                                            XN[:, i, :], None).then_inc(S("rows_out"), 16)

            pool.wait_ge(S("deg_out_made"), T)
            link(pool.tensor_scalar(inv_in[:, :], deg_in[:, :], 1.0, None, ALU.max))
            link(pool.tensor_scalar(inv_out[:, :], deg_out[:, :], 1.0, None, ALU.max))
            pool.tensor_tensor(inv_in[:, :], inv_in[:, :], half_pow[0:P, :], ALU.pow)
            pool.tensor_tensor(inv_out[:, :], inv_out[:, :], half_pow[0:P, :], ALU.pow).then_inc(S("degi_made"), 1)

            def inverse_rms(n, step, made, k):
                pool.wait_ge(step, n)
                pool.tensor_tensor(rms[:, k:k + 1], ssum[:, k:k + 1], half_pow[:, 0:1], ALU.pow).then_inc(made, 1)
            with pool.Fori(0, MT0 // LANES) as g:
                for k in range(LANES):
                    inverse_rms(g * LANES + k + 1, S("rms_step"), S("rms_made"), k)
                for k in range(LANES):
                    inverse_rms(g * LANES + k + 1, S("rms2_step"), S("rms2_made"), k)
            for k in range(LANES):
                pool.wait_ge(y_out[k], 16 * (MT0 // LANES))
            pool.wait_ge(S("y_made"), MT0)

            def rstd_tile(waited, n, i, scale, made):
                r = rstd[0:P, i:i + 1]
                pool.wait_ge(waited, n)
                link(pool.tensor_scalar(r, mv[0:P, i, 1:2], 1.0, LN_EPS, ALU.mult, ALU.add))
                if scale is None:
                    pool.tensor_tensor(r, r, half_pow[0:P, 0:1], ALU.pow).then_inc(made, 1)
                else:
                    link(pool.tensor_tensor(r, r, half_pow[0:P, 0:1], ALU.pow))
                    pool.tensor_tensor(r, r, scale, ALU.mult).then_inc(made, 1)
            for i in range(T + 4):
                if i > 3:
                    n = i - 4
                    rstd_tile(S("ln_stat"), 2 * T + n + 1, n, inv_out[:, n:n + 1], S("ln_rstd"))
                for k in range(K0 if i < T else 0):
                    pool.indirect_dma_start(rows[K0 * i + k], None, made0_d,
                                            bass.IndirectOffsetOnAxis(ap=slot[:, k, i:i + 1], axis=0))\
                        .then_inc(rows_in[i], 16)

            def next_norms(j):
                rstd_tile(S("ln_stat"), 3 * T + 2 * j + 1, j, None, S("ln_rstd"))
                rstd_tile(S("ln_stat"), 3 * T + 2 * j + 2, j, None, S("ln_rstd"))
            for j in range(T):
                if j > 1:
                    next_norms(j - 2)
                rstd_tile(S("hg_stat"), j + 1, j, None, S("hg_rstd"))
            next_norms(T - 2)
            next_norms(T - 1)
            pool.wait_ge(S("slot1_made"), 1)
            pool.wait_ge(S("xn_made"), 4 * T)
            for i in range(T):
                pool.indirect_dma_start(slots1_d, bass.IndirectOffsetOnAxis(ap=slot[:, 0, i:i + 1], axis=0),
                                        XN[:, i, :], None).then_inc(S("rows1_out"), 16)
            for k in range(LANES):
                pool.wait_ge(yy_out[k], 16 * (MT1 // LANES))
            pool.wait_ge(S("yy_made"), MT1)
            for i in range(T):
                pool.indirect_dma_start(rows[i], None, made1_d,
                                        bass.IndirectOffsetOnAxis(ap=slot[:, 0, i:i + 1], axis=0))\
                    .then_inc(rows_in[i], 16)

        @block.vector
        def _(dve):
            c = [0]

            def link(ins):
                c[0] += 1
                ins.then_inc(S("dve_chain"), 1)
                dve.wait_ge(S("dve_chain"), c[0])

            dve.wait_ge(S("edges_in"), 32)
            dve.tensor_copy(idx_f[:, 0, :], raw_idx[:, 0, :]).then_inc(S("idx_step"), 1)
            dve.tensor_copy(src_f, raw_idx[:, 1, :]).then_inc(S("idx_step"), 1)
            dve.wait_ge(S("idx_step"), 2)
            dve.tensor_scalar(upper, src_f, float(HALF), None, ALU.is_ge).then_inc(S("idx_step"), 1)
            dve.wait_ge(S("idx_step"), 3)
            dve.scalar_tensor_tensor(idx_f[:, 1, :], upper, -float(HALF), src_f, ALU.mult, ALU.add)\
               .then_inc(S("idx_step"), 1)
            dve.tensor_scalar(idx_f[:, 2, :], upper, float(2 ** SHIFT - 1), 1.0, ALU.mult, ALU.add)\
               .then_inc(S("idx_step"), 1)
            for k, op in ((0, ALU.min), (2, ALU.max)):
                ins = dve.tensor_reduce(bounds[:, k:k + 2],
                                        idx_f[:, 0, :].rearrange("p (r e) -> p r e", r=2), X_AXIS, op)
                link(ins)
            dve.wait_ge(S("consts"), 1)
            for k in range(4):
                dve.tensor_scalar(span_diag[:, k, :], ident[0:80, 0:80], bounds[:, k:k + 1], None, ALU.mult)\
                   .then_inc(S("diag_made"), 1)
            dve.wait_ge(S("idx_turned"), 1)
            link(dve.tensor_copy(idxT.rearrange("p k (q r) -> p k r q", r=2),
                                 bank(6, EP, 480).rearrange("p (k r q) -> p k r q", k=3, r=2)))
            dve.wait_ge(S("span_sums"), 1)
            least, greatest = bank(7, T, ET), bank(7, T, ET, ET)
            def step(ins, n):
                ins.then_inc(S("span_step"), 1)
                dve.wait_ge(S("span_step"), n)
            step(dve.tensor_scalar(span_tmp[:, 2, :], least, spans[:, 1:2], None, ALU.is_lt), 1)
            step(dve.scalar_tensor_tensor(span_tmp[:, 2, :], greatest, spans[:, 0:1], span_tmp[:, 2, :],
                                          ALU.is_ge, ALU.mult), 2)
            step(dve.scalar_tensor_tensor(span_tmp[:, 3, :], span_tmp[:, 2, :], -BIG, span_tmp[:, 1, :],
                                          ALU.mult, ALU.add), 3)
            dve.tensor_tensor(span_tmp[:, 4, :], span_tmp[:, 2, :], span_tmp[:, 0, :], ALU.mult)
            step(dve.tensor_reduce(spans[:, 2:3], span_tmp[:, 3, :], X_AXIS, ALU.min), 4)
            step(dve.tensor_reduce(spans[:, 3:4], span_tmp[:, 4, :], X_AXIS, ALU.max), 5)
            step(dve.tensor_tensor(spans[:, 4:5], spans[:, 3:4], spans[:, 2:3], ALU.subtract), 6)
            step(dve.tensor_scalar(spans[:, 6:7], spans[:, 2:3], float(ET - WIN), 0.0, ALU.min, ALU.max), 7)
            step(dve.tensor_scalar(spans[:, 7:8], spans[:, 4:5], float(WIN - 1), None, ALU.is_le), 8)
            dve.wait_ge(S("ctl_sums"), 1)
            link(dve.tensor_copy(ctl_f[:, 0:T], bank(7, 1, T, 320)))
            link(dve.tensor_reduce(ctl_f[:, T:T + 1], bank(7, 1, T, 336), X_AXIS, ALU.min))
            dve.tensor_copy(ctl[:, 0:T + 1], ctl_f[:, 0:T + 1]).then_inc(S("ctl_ready"), 1)

            def row_stats(source, i):
                link(dve.bn_stats(stats[0:P, i, :], source[:, i, :]))
                dve.bn_aggr(mv[0:P, i, :], stats[0:P, i, :]).then_inc(S("ln_stat"), 1)

            def layer_norm_stats(source):
                for i in range(T):
                    row_stats(source, i)

            def layer_norm_rows(n, source):
                dve.wait_ge(S("ln_rstd"), n)
                for i in range(T):
                    dve.tensor_scalar(XN[:, i, :], source[:, i, :], mv[0:P, i, 0:1], rstd[0:P, i:i + 1],
                                      ALU.subtract, ALU.mult).then_inc(S("xn_made"), 1)
            dve.wait_ge(S("x_in"), 16)
            layer_norm_stats(X)
            layer_norm_rows(1, X)

            dve.wait_ge(S("ctl_ready"), 1)
            all_hold = dve.value_load(ctl[0:1, T:T + 1], min_val=0, max_val=1)

            def unpack(b, source_sem, source_n):
                dve.wait_ge(source_sem, source_n)
                above_zero(dve, S("ct_made"), b)
                dve.tensor_scalar(unpacked[:, 0:HALF], packed, 2 ** SHIFT - 1, None, ALU.bitwise_and)
                dve.tensor_scalar(unpacked[:, HALF:N], packed, SHIFT, None, ALU.logical_shift_right)\
                   .then_inc(S("unpacked_out"), 1)

            def floor_one(b):
                dve.wait_ge(S("ct_made"), b + 1)
                dve.tensor_scalar(lnCT, CT, 1.0, None, ALU.max).then_inc(S("max_made"), 1)
                dve.tensor_scalar(penalty, CT, 0.5, NEG, ALU.is_lt, ALU.mult).then_inc(S("pen_made"), 1)

            def log_counts(b):
                dve.wait_ge(S("ln_made"), b + 1)
                dve.wait_ge(S("pen_made"), b + 1)
                dve.tensor_tensor(lnCT, lnCT, penalty, ALU.add).then_inc(S("lnct_made"), 1)

            def hot_group(g0, w0, hot, free):
                for k in range(GROUP):
                    dve.wait_ge(free, g0 + k + 1)
                    dve.tensor_scalar(oh_dst[:, k, :], iota_dst, win[:, 0, w0 + k:w0 + k + 1], None, ALU.is_equal)
                    dve.tensor_scalar(oh_src[:, k, :], iota_src, win[:, 1, w0 + k:w0 + k + 1],
                                      win[:, 2, w0 + k:w0 + k + 1], ALU.is_equal, ALU.mult).then_inc(hot, 1)

            def make_window(b, start, tiles, made, n):
                off = tile_off[0:EP, bass.ds(b, 1)] if not isinstance(b, int) else tile_off[0:EP, b:b + 1]
                dve.tensor_scalar(win[:, 0, 0:tiles], idxT[:, 0, bass.ds(start, tiles)], off, None, ALU.subtract)
                dve.tensor_copy(win[:, 1:3, 0:tiles], idxT[:, 1:3, bass.ds(start, tiles)]).then_inc(made, 1)
                dve.wait_ge(made, n)

            def fast_block(b, after):
                start = dve.value_load(ctl[0:1, bass.ds(b, 1)], min_val=0, max_val=ET - WIN)
                above_zero(dve, S("hot"), b * WIN)
                make_window(b, start, WIN, S("win_made"), b + 1)
                for w0 in range(0, WIN, GROUP):
                    hot_group(b * WIN + w0, w0, S("hot"), S("slots_free"))
                    if after is not None and w0 == 0:
                        unpack(after, S("packed_out"), after + 1)
                    if after is not None and w0 == 8:
                        floor_one(after)
                    if after is not None and w0 == 16:
                        log_counts(after)
            with dve.If(all_hold):
                fast_block(0, None)
                fast_block(1, 0)
                with dve.Fori(2, T) as b:
                    fast_block(b, b - 1)
                unpack(T - 1, S("packed_out"), T)
                floor_one(T - 1)
                log_counts(T - 1)
            with dve.Else():
                NW = ET // GEN_WIN
                with dve.Fori(0, T) as b:
                    for w in range(NW):
                        if w:
                            dve.wait_ge(S("gen_hot"), b * ET + w * GEN_WIN)
                        make_window(b, w * GEN_WIN, GEN_WIN, S("gen_win"), b * NW + w + 1)
                        for w0 in range(0, GEN_WIN, GROUP):
                            hot_group(b * ET + w * GEN_WIN + w0, w0, S("gen_hot"), S("gen_free"))
                        dve.wait_ge(S("gen_free"), b * ET + w * GEN_WIN + (GEN_WIN + GROUP))
                        gs = b * (4 * NW) + 4 * w

                        def gstep(ins, n):
                            ins.then_inc(S("gen_fold"), 1)
                            dve.wait_ge(S("gen_fold"), gs + n)
                        gstep(dve.tensor_copy(packed, ps[0:P, 0:HALF]), 1)
                        gstep(dve.tensor_scalar(unpacked[:, 0:HALF], packed, 2 ** SHIFT - 1, None, ALU.bitwise_and), 2)
                        gstep(dve.tensor_scalar(unpacked[:, HALF:N], packed, SHIFT, None, ALU.logical_shift_right), 3)
                        if w == 0:
                            dve.tensor_copy(sumCT, unpacked).then_inc(S("gen_fold"), 1)
                        else:
                            dve.tensor_tensor(sumCT, sumCT, unpacked, ALU.add).then_inc(S("gen_fold"), 1)
                        dve.wait_ge(S("gen_fold"), gs + 4)
                        if w < NW - 1:
                            dve.nop().then_inc(S("gen_step"), 1)
                    dve.tensor_copy(unpacked, sumCT).then_inc(S("unpacked_out"), 1)
                    dve.nop().then_inc(S("gen_step"), 1)
                    floor_one(b)
                    log_counts(b)
                    dve.wait_ge(S("lnct_turned"), 3 * b + 3)
            dve.end_ifs()

            for i in range(T):
                dve.wait_ge(S("v_turned"), i + 1)
                if i == 0:
                    dve.wait_ge(S("xt_turned"), T)
                dve.tensor_copy(XN[:, i, :], bank(i % 2, P)).then_inc(S("v_moved"), 1)
            dve.wait_ge(S("lnct_moved"), 3 * T)

            def await_scores(u, tb, nth_logs, h):
                if h == 0:
                    dve.wait_ge(logs_in[tb], nth_logs)
                dve.wait_ge(S("s_made"), u + 1)
                above_zero(dve, S("p_made"), u - 1)

            def negate_scores(tb, h):
                buf = h % 2
                dve.tensor_tensor_reduce(SC[buf], ps[0:P, 1536 * buf:1536 * buf + N], LNB[tb],
                                         -1.0, 3.0e38, ALU.add, ALU.min, neg_max[:, h % 4:h % 4 + 1]).then_inc(S("z_made"), 1)

            def move_turned(u, h):
                buf = h % 2
                a, z = TPIECES[1]
                dve.wait_ge(S("p_turned"), 3 * u + 2)
                above_zero(dve, S("o_made"), u - 1)
                dve.tensor_copy(PT[buf][:, a:z, :], bank(7, P, (z - a) * P).rearrange("p (i n) -> p i n", n=P))\
                   .then_inc(S("pt_moved_v"), 1)

            def inverse_den(u, h):
                buf = h % 2
                dve.wait_ge(S("p_made"), u + 1)
                above_zero(dve, S("o_moved"), u - 1)
                dve.reciprocal(rden[:, buf:buf + 1], den[:, buf:buf + 1]).then_inc(S("rden_made"), 1)
                dve.wait_ge(S("rden_made"), 2 * u + 1)
                dve.scalar_tensor_tensor(rden[:, buf:buf + 1], neg_max[:, h % 4:h % 4 + 1], -0.1 * NEG,
                                         rden[:, buf:buf + 1], ALU.is_lt, ALU.mult).then_inc(S("rden_made"), 1)

            def out_degree(i):
                dve.wait_ge(count_rows_in[i % 4], 16 * (i // 4) + 16)
                dve.tensor_reduce(deg_out[:, i:i + 1], count_rows[i % 4], X_AXIS, ALU.add)\
                   .then_inc(S("deg_out_made"), 1)

            def attend(i, tb, nth_logs, last=False, norm=(), degrees=()):
                for h in range(HEADS):
                    u = i * HEADS + h
                    more = not (last and h >= HEADS - 2)
                    nxt = (tb, nth_logs, h + 2) if h < HEADS - 2 else (1 - tb, nth_logs + 16 * tb, h + 2 - HEADS)
                    move_turned(u, h)
                    if more:
                        await_scores(u + 2, *nxt)
                    inverse_den(u, h)
                    if more:
                        negate_scores(nxt[0], nxt[2])
                    if h < len(degrees):
                        out_degree(degrees[h])
                    if h < len(norm):
                        dve.wait_ge(S("x_added"), (norm[h] + 1) * HEADS)
                        row_stats(X, norm[h])
            dve.wait_ge(S("counts_out"), 16 * T)
            await_scores(0, 0, 16, 0)
            negate_scores(0, 0)
            await_scores(1, 0, 16, 1)
            negate_scores(0, 1)
            attend(0, 0, 16, degrees=range(5))
            attend(1, 1, 16, degrees=range(5, T))
            with dve.Fori(1, T // 2 - 1) as ii:
                attend(2 * ii, 0, 16 * ii + 16)
                attend(2 * ii + 1, 1, 16 * ii + 16)
            attend(T - 2, 0, 8 * T, norm=range(T - 2))
            attend(T - 1, 1, 8 * T, last=True, norm=(T - 2,))
            dve.wait_ge(S("x_added"), T * HEADS)

            def two_best():
                for i in range(T):
                    ins = dve.max(top[:, i, :], logits[:, i, :])
                link(ins)
                for i in range(T):
                    ins = dve.max_index(top_i[:, i, :], top[:, i, :], logits[:, i, :])
                link(ins)

            row_stats(X, T - 1)
            layer_norm_rows(2, X)
            dve.wait_ge(S("log_made"), 1)
            link(dve.tensor_copy(logits[:, :, :], bank(2, P, 8 * T).rearrange("p (i e) -> p i e", e=8)))
            two_best()
            link(dve.tensor_copy(pick[:, :, :], top_i[:, :, 0:2]))
            dve.tensor_tensor(gates[:, 0, :], top[:, :, 1], top[:, :, 0], ALU.subtract).then_inc(S("gate_step"), 1)
            iota_b = iota8[:, :].unsqueeze(1).to_broadcast([P, T, 8])
            for k in range(K0):
                dve.tensor_tensor(mask[:, k, :, :], iota_b, pick[:, :, k:k + 1].to_broadcast([P, T, 8]),
                                  ALU.is_equal).then_inc(S("mask_made"), 1)
            dve.wait_ge(S("mask_made"), 2)
            dve.tensor_tensor(mask[:, 2, :, :], mask[:, 0, :, :], mask[:, 1, :, :], ALU.add)\
               .then_inc(S("mask_made"), 1)
            dve.wait_ge(S("gate_exp"), 1)
            link(dve.tensor_scalar(gates[:, 1, :], gates[:, 0, :], 1.0, None, ALU.add))
            link(dve.reciprocal(gates[:, 2, :], gates[:, 1, :]))
            link(dve.tensor_tensor(gates[:, 3, :], gates[:, 0, :], gates[:, 2, :], ALU.mult))

            def slots_of(masks, tiles, experts, made):
                tot = bank(3, 128, 8 * T, 128).rearrange("p (i e) -> p i e", e=8)
                link(dve.memset(place[:, 0, :], 0.0))
                for i in range(1, T):
                    link(dve.tensor_tensor(place[:, i, :], place[:, i - 1, :], tot[:, i - 1, :], ALU.add))
                link(dve.tensor_tensor(cnt[:, 0, :], place[:, T - 1, :], tot[:, T - 1, :], ALU.add))
                link(dve.tensor_scalar(cnt_i[:, :], cnt[:, 0, :], float(TM - 1), None, ALU.add))
                link(dve.tensor_scalar(cnt_i[:, :], cnt_i[:, :], 7, None, ALU.logical_shift_right))
                link(dve.tensor_copy(cnt[:, 1, :], cnt_i[:, :]))
                link(dve.memset(cnt[:, 4, :], 1.0))
                link(dve.tensor_tensor_scan(cnt[:, 2, :], cnt[:, 4, :], cnt[:, 1, :], 0.0, ALU.mult, ALU.add))
                link(dve.tensor_tensor(cnt[:, 3, :], cnt[:, 2, :], cnt[:, 1, :], ALU.subtract))
                link(dve.tensor_scalar(cnt[:, 3, :], cnt[:, 3, :], float(TM), None, ALU.mult))
                link(dve.tensor_tensor(place[0:P, :, :], place[0:P, :, :],
                                       bank(3, P, 8 * T).rearrange("p (i e) -> p i e", e=8), ALU.add))
                link(dve.tensor_tensor(place[0:P, :, :], place[0:P, :, :],
                                       cnt[0:P, 3:4, :].to_broadcast([P, T, 8]), ALU.add))
                for k, m in enumerate(masks):
                    link(dve.tensor_tensor(logits[:, :, :], m, place[0:P, :, :], ALU.mult))
                    link(dve.tensor_reduce(slot_f[:, k, :], logits[:, :, :], X_AXIS, ALU.add))
                    link(dve.tensor_copy(slot[:, k, :], slot_f[:, k, :]))
                link(dve.tensor_tensor(owner[:, 0:tiles, :], iotaT[:, 0:tiles].unsqueeze(2).to_broadcast([1, tiles, 8]),
                                       cnt[0:1, 2:3, :].to_broadcast([1, tiles, 8]), ALU.is_ge))
                link(dve.tensor_reduce(owner_f[:, 0:tiles], owner[:, 0:tiles, :], X_AXIS, ALU.add))
                link(dve.tensor_scalar(owner_f[:, 0:tiles], owner_f[:, 0:tiles], float(experts - 1), None, ALU.min))
                dve.tensor_copy(owner_i[:, 0:tiles], owner_f[:, 0:tiles]).then_inc(made, 1)
                dve.wait_ge(made, 1)
            dve.wait_ge(S("rank_made"), 1)
            slots_of([mask[:, 0, :, :], mask[:, 1, :, :]], MT0, E0, S("slot_made"))
            dve.wait_ge(S("nrm_in"), 32)

            def mix0(g):
                lanes_ = range(LANES)
                e = [dve.value_load(owner_i[0:1, bass.ds(g * LANES + k, 1)], min_val=0, max_val=E0 - 1)
                     for k in lanes_]
                for k in lanes_:
                    n = g * LANES + k + 1
                    dve.wait_ge(S("g1_made"), n)
                    dve.tensor_tensor_reduce(sq[k], act1[k], act1[k], 1.0, 0.0, ALU.mult, ALU.add,
                                             ssum[:, k:k + 1]).then_inc(S("ss_made"), 1)
                    dve.wait_ge(S("ss_made"), n)
                    dve.tensor_scalar(ssum[:, k:k + 1], ssum[:, k:k + 1], 1.0 / H0, RMS_EPS, ALU.mult, ALU.add)\
                       .then_inc(S("rms_step"), 1)
                for k in lanes_:
                    n = g * LANES + k + 1
                    dve.wait_ge(S("rms_made"), n)
                    dve.scalar_tensor_tensor(h1n[k], act1[k], rms[:, k:k + 1], N1B[:, bass.ds(e[k] * H0, H0)],
                                             ALU.mult, ALU.mult).then_inc(S("n1_made"), 1)
                for k in lanes_:
                    n = g * LANES + k + 1
                    dve.wait_ge(S("g2_made"), n)
                    dve.tensor_tensor_reduce(sq[k], act1[k], act1[k], 1.0, 0.0, ALU.mult, ALU.add,
                                             ssum[:, k:k + 1]).then_inc(S("ss2_made"), 1)
                    dve.wait_ge(S("ss2_made"), n)
                    dve.tensor_scalar(ssum[:, k:k + 1], ssum[:, k:k + 1], 1.0 / H0, RMS_EPS, ALU.mult, ALU.add)\
                       .then_inc(S("rms2_step"), 1)
                for k in lanes_:
                    n = g * LANES + k + 1
                    dve.wait_ge(S("rms2_made"), n)
                    dve.scalar_tensor_tensor(h2n[k], act1[k], rms[:, k:k + 1], N2B[:, bass.ds(e[k] * H0, H0)],
                                             ALU.mult, ALU.mult).then_inc(S("h2_scaled"), 1)
                    dve.wait_ge(S("h2_scaled"), n)
                    dve.tensor_tensor(h2n[k], h2n[k], h1n[k], ALU.add).then_inc(S("n2_made"), 1)
                for k in lanes_:
                    n = g * LANES + k + 1
                    dve.wait_ge(S("y_made"), n)
                    above_zero(dve, y_out[k], g * 16)
                    dve.tensor_copy(ys[k], bank(2 * k + 1)).then_inc(S("y_moved"), 1)
            mix0(0)
            with dve.Fori(1, MT0 // LANES) as g:
                mix0(g)

            def add_rows(i, n, gate, nth):
                dve.scalar_tensor_tensor(X[:, i, :], rows[n], gate, X[:, i, :],
                                         ALU.mult, ALU.add).then_inc(S("rows_added"), 1)
                dve.wait_ge(S("rows_added"), nth)

            def rows_over_root(i):
                dve.wait_ge(S("ln_rstd"), 2 + i + 1)
                dve.tensor_scalar(HS[i], X[:, i, :], mv[0:P, i, 0:1], rstd[0:P, i:i + 1],
                                  ALU.subtract, ALU.mult).then_inc(S("hs_made"), 1)
            for i in range(T):
                dve.wait_ge(rows_in[i], 16 * K0)
                for k in range(K0):
                    add_rows(i, K0 * i + k, gates[:, 2 + k, i:i + 1], K0 * i + k + 1)
                row_stats(X, i)
                if i:
                    rows_over_root(i - 1)
            rows_over_root(T - 1)

            dve.wait_ge(S("degi_made"), 1)
            dve.wait_ge(S("vec_in"), 48)

            def finish(j):
                b = j % 2
                dve.wait_ge(S("hg_made"), j + 1)
                dve.tensor_tensor(HG[b], bank(4 + b, P), BIAS[0:P, :], ALU.add).then_inc(S("hg_biased"), 1)
                dve.wait_ge(S("hg_biased"), j + 1)
                link(dve.bn_stats(stats[0:P, j, :], HG[b]))
                dve.bn_aggr(mv[0:P, j, :], stats[0:P, j, :]).then_inc(S("hg_stat"), 1)
                dve.wait_ge(S("hg_stat"), j + 1)
                dve.wait_ge(S("hg_rstd"), j + 1)
                link(dve.tensor_scalar(HG[b], HG[b], mv[0:P, j, 0:1], rstd[0:P, j:j + 1], ALU.subtract, ALU.mult))
                link(dve.tensor_tensor(HG[b], HG[b], GAMMA[0:P, :], ALU.mult))
                dve.tensor_tensor(HG[b], HG[b], BETA[0:P, :], ALU.add).then_inc(S("hg_shift"), 1)

            def add_layer(j):
                dve.wait_ge(S("hg_gelu"), j + 1)
                link(dve.tensor_tensor(X[:, j, :], X[:, j, :], HG[j % 2], ALU.add))
                row_stats(X, j)
                dve.wait_ge(S("ln_rstd"), 2 + T + 2 * j + 1)
                dve.tensor_scalar(XM[j], X[:, j, :], mv[0:P, j, 0:1], rstd[0:P, j:j + 1],
                                  ALU.subtract, ALU.mult).then_inc(S("xn_made"), 1)
                dve.wait_ge(S("xn_made"), 2 * T + j + 1)
                link(dve.bn_stats(stats[0:P, j, :], XM[j]))
                dve.bn_aggr(mv[0:P, j, :], stats[0:P, j, :]).then_inc(S("ln_stat"), 1)
            for j in range(T):
                dve.wait_ge(S("agg_made"), j + 1)
                above_zero(dve, S("agg_turned"), j - 1)
                dve.tensor_scalar(AGG[j % 2], bank(j % 2, P), inv_in[:, j:j + 1], None, ALU.mult)\
                   .then_inc(S("agg_moved"), 1)
                if j:
                    if j > 2:
                        add_layer(j - 3)
                    finish(j - 1)
            add_layer(T - 3)
            finish(T - 1)
            add_layer(T - 2)
            add_layer(T - 1)

            dve.wait_ge(S("agg_made"), T)
            dve.wait_ge(S("ln_rstd"), 2 + 3 * T)
            dve.wait_ge(S("gam_in"), 16)
            for i in range(T):
                link(dve.tensor_scalar(XN[:, i, :], XM[i], mv[0:P, i, 0:1], rstd[0:P, i:i + 1],
                                       ALU.subtract, ALU.mult))
                dve.tensor_tensor(XN[:, i, :], XN[:, i, :], GAM1[0:P, :], ALU.mult).then_inc(S("xn_made"), 1)
            dve.wait_ge(S("log1_made"), 1)
            link(dve.memset(logits[:, :, :], -3.0e38))
            dve.tensor_copy(logits[:, :, 0:E1], bank(2, P, 8 * T).rearrange("p (i e) -> p i e", e=8)[:, :, 0:E1])\
               .then_inc(S("g1_step"), 1)
            dve.wait_ge(S("g1_step"), 1)
            two_best()
            link(dve.tensor_copy(pick[:, :, :], top_i[:, :, 0:2]))
            dve.tensor_tensor(mask[:, 0, :, :], iota_b, pick[:, :, 0:1].to_broadcast([P, T, 8]),
                              ALU.is_equal).then_inc(S("log1_top"), 1)
            dve.tensor_tensor(logits[:, :, 0:E1], logits[:, :, 0:E1], top[:, :, 0:1].to_broadcast([P, T, E1]),
                              ALU.subtract).then_inc(S("g1_step"), 1)
            link(dve.tensor_tensor(gates[:, 1, :], top[:, :, 1], top[:, :, 0], ALU.subtract))
            dve.tensor_copy(logits[:, :, 6:7], gates[:, 1, :].unsqueeze(2)).then_inc(S("g1_step"), 1)
            dve.wait_ge(S("g1_exp"), 1)
            link(dve.tensor_reduce(gates[:, 0, :], logits[:, :, 0:E1], X_AXIS, ALU.add))
            link(dve.reciprocal(gates[:, 2, :], gates[:, 0, :]))
            dve.wait_ge(S("log1_top"), 1)
            link(dve.tensor_scalar(mask[:, 1, :, :], mask[:, 0, :, :], -1.0, 1.0, ALU.mult, ALU.add))
            link(dve.tensor_tensor(mask[:, 1, :, 0:E1], mask[:, 1, :, 0:E1], logits[:, :, 0:E1], ALU.mult))
            link(dve.tensor_reduce(gates[:, 1, :], mask[:, 1, :, 0:E1], X_AXIS, ALU.max))
            link(dve.tensor_tensor(gates[:, 1, :], gates[:, 1, :], gates[:, 2, :], ALU.mult))
            link(dve.tensor_tensor(gates[:, 1, :], gates[:, 1, :], gates[:, 2, :], ALU.add))
            link(dve.tensor_scalar(gates[:, 1, :], gates[:, 1, :], GATE_EPS, None, ALU.add))
            link(dve.reciprocal(gates[:, 3, :], gates[:, 1, :]))
            link(dve.tensor_tensor(gates[:, 0, :], gates[:, 2, :], gates[:, 3, :], ALU.mult))
            dve.wait_ge(S("rank1_made"), 1)
            slots_of([mask[:, 0, :, :]], MT1, E1, S("slot1_made"))

            def mix1(g):
                for k in range(LANES):
                    dve.wait_ge(S("yy_made"), g * LANES + k + 1)
                    above_zero(dve, yy_out[k], g * 16)
                    dve.tensor_copy(ys[k], bank(2 * k + 1)).then_inc(S("yy_moved"), 1)
            mix1(0)
            with dve.Fori(1, MT1 // LANES) as g:
                mix1(g)
            for i in range(T):
                dve.wait_ge(rows_in[i], 16 * (K0 + 1))
                add_rows(i, i, gates[:, 0, i:i + 1], K0 * T + i + 1)
                dve.nop().then_inc(S("x_stored"), 1)


_INS = ["x", "src", "dst", "L0_gnn_W", "L0_ffn_gate_w", "L0_ffn_w1", "L0_ffn_w2", "L0_ffn_w3", "L0_ffn_n1",
        "L0_ffn_n2", "L1_gnn_W", "L1_gnn_b", "L1_gnn_gamma", "L1_gnn_beta", "L1_ffn_w_gating", "L1_ffn_gamma",
        "L1_ffn_w1", "L1_ffn_w2"]
_OUTS = [((N, D), "float32")]


def kernel(**inputs):
    import numpy as _np
    import concourse.bacc as _bacc
    from concourse import mybir as _mybir
    from concourse.bass_utils import run_bass_kernel_spmd as _run

    nc = _bacc.Bacc("TRN2", target_bir_lowering=False, num_devices=1)
    arrays, args = {}, []
    for name in _INS:
        a = _np.ascontiguousarray(inputs[name])
        arrays[f"in_{name}_dram"] = a
        args.append(nc.dram_tensor(f"in_{name}_dram", a.shape, _mybir.dt.from_np(a.dtype), kind="ExternalInput").ap())
    for i, (shape, dtype) in enumerate(_OUTS):
        dt = _mybir.dt.from_np(_np.dtype(dtype))
        args.append(nc.dram_tensor(f"out_{i}_dram", shape, dt, kind="ExternalOutput").ap())
    gnn_moe_kernel(nc, *args)
    r = _run(nc, [arrays], core_ids=[0])
    return r.results[0]["out_0_dram"]
```
